# Optimizing a Trainium2 kernel written in Bass

```python
import numpy as np
import jax
import jax.numpy as jnp

def _softmax(x, axis=-1):
    return jax.nn.softmax(x, axis=axis)

def _gelu(x):
    return jax.nn.gelu(x, approximate=True)

def _silu(x):
    return jax.nn.silu(x)

def _sigmoid(x):
    return jax.nn.sigmoid(x)

def _layernorm(x, axis=-1, eps=1e-05):
    m = jnp.mean(x, axis=axis, keepdims=True)
    v = jnp.var(x, axis=axis, keepdims=True)
    return (x - m) / jnp.sqrt(v + eps)

def _scatter_add(tgt, idx, src, axis=0):
    return tgt.at[idx].add(src)

def _segment_sum(src, seg, n):
    return jax.ops.segment_sum(src, seg, n)
kernel_name = 'mk_gnn_resnorm_d2_gnn_r32_b10e23'

def setup_inputs(seed: int=0):
    np.random.seed(seed)
    _w = jnp.asarray

    def _rec_inputs():
        import jax
        import jax.numpy as jnp
        _gk = jax.random.key(seed)
        x = -0.0002117 + 1 * jax.random.normal(jax.random.fold_in(_gk, 1), (3125, 256), jnp.float32)
        src = jax.random.randint(jax.random.fold_in(_gk, 2), (50000,), 0, 3125, jnp.int32)
        dst = jnp.minimum((3125 * jax.random.uniform(jax.random.fold_in(_gk, 3), (50000,)) ** 2.0).astype(jnp.int32), 99999)
        _o = jnp.argsort(dst, stable=True)
        src = src[_o]
        dst = dst[_o]
        edge_attr_64 = 0.000102155 + 1.00015 * jax.random.normal(jax.random.fold_in(_gk, 12), (50000, 64), jnp.float32)
        edge_weight = jax.random.uniform(jax.random.fold_in(_gk, 14), (50000,), jnp.float32, 0.0, 1)
        return (x, src, dst, edge_attr_64, edge_weight)
    x, src, dst, edge_attr_64, edge_weight = _rec_inputs()

    def _L0_gnn_setup():
        import jax, jax.numpy as jnp
        import numpy as np
        N_NODES = 3125
        N_EDGES = 100000
        D_IN = 256
        UNITS = 256
        key = jax.random.key(seed)
        k1, k2, k3, k4, k5 = jax.random.split(key, 5)
        x = jax.random.normal(k1, (N_NODES, D_IN), dtype=jnp.float32)
        edge_row = jax.random.randint(k2, (N_EDGES,), 0, N_NODES, dtype=jnp.int64)
        edge_col = jax.random.randint(k3, (N_EDGES,), 0, N_NODES, dtype=jnp.int64)
        edge_val = jax.random.uniform(k4, (N_EDGES,), dtype=jnp.float32)
        kernel = jax.random.normal(k5, (D_IN, UNITS), dtype=jnp.float32) * (1.0 / np.sqrt(D_IN))
        bias = jnp.zeros((UNITS,), dtype=jnp.float32)
        return {'x': x, 'edge_row': edge_row, 'edge_col': edge_col, 'edge_val': edge_val, 'kernel': kernel, 'bias': bias}
    _L0_gnn_all = _L0_gnn_setup()
    _L0_gnn_in = {k: v for k, v in _L0_gnn_all.items() if k in ('kernel', 'bias')}
    del _L0_gnn_all

    def _L1_gnn_setup():
        import jax, jax.numpy as jnp
        import numpy as np
        N_NODES = 50000
        N_EDGES = 15625
        HDIM = 256
        EDIM = 64
        MSG_H = 512
        UPD_H = 512
        LN_EPS = 1e-05

        def _mlp(x, W1, b1, W2, b2):
            return jax.nn.relu(x @ W1 + b1) @ W2 + b2

        def _layer_norm(x, gamma, beta):
            mu = jnp.mean(x, axis=-1, keepdims=True)
            var = jnp.mean(jnp.square(x - mu), axis=-1, keepdims=True)
            return (x - mu) * jax.lax.rsqrt(var + LN_EPS) * gamma + beta
        key = jax.random.key(seed)
        ks = jax.random.split(key, 12)

        def lin_init(k, fan_in, fan_out):
            bound = 1.0 / np.sqrt(fan_in)
            return jax.random.uniform(k, (fan_in, fan_out), jnp.float32, -bound, bound)
        h = jax.random.normal(ks[0], (N_NODES, HDIM), jnp.float32)
        edge_index = jax.random.randint(ks[1], (2, N_EDGES), 0, N_NODES, jnp.int64)
        edge_attr = jax.random.normal(ks[2], (N_EDGES, EDIM), jnp.float32)
        eW1 = lin_init(ks[3], 2 * HDIM + EDIM, MSG_H)
        eb1 = jnp.zeros((MSG_H,), jnp.float32)
        eW2 = lin_init(ks[4], MSG_H, HDIM)
        eb2 = jnp.zeros((HDIM,), jnp.float32)
        nW1 = lin_init(ks[5], 2 * HDIM, UPD_H)
        nb1 = jnp.zeros((UPD_H,), jnp.float32)
        nW2 = lin_init(ks[6], UPD_H, HDIM)
        nb2 = jnp.zeros((HDIM,), jnp.float32)
        ln_gamma = jnp.ones((HDIM,), jnp.float32)
        ln_beta = jnp.zeros((HDIM,), jnp.float32)
        return {'h': h, 'edge_index': edge_index, 'edge_attr': edge_attr, 'eW1': eW1, 'eb1': eb1, 'eW2': eW2, 'eb2': eb2, 'nW1': nW1, 'nb1': nb1, 'nW2': nW2, 'nb2': nb2, 'ln_gamma': ln_gamma, 'ln_beta': ln_beta}
    _L1_gnn_all = _L1_gnn_setup()
    _L1_gnn_in = {k: v for k, v in _L1_gnn_all.items() if k in ('eW1', 'eb1', 'eW2', 'eb2', 'nW1', 'nb1', 'nW2', 'nb2', 'ln_gamma', 'ln_beta')}
    del _L1_gnn_all
    return {'x': x, 'src': src, 'dst': dst, 'edge_attr_64': edge_attr_64, 'edge_weight': edge_weight, 'L0_gnn_kernel': _L0_gnn_in['kernel'], 'L0_gnn_bias': _L0_gnn_in['bias'], 'L1_gnn_eW1': _L1_gnn_in['eW1'], 'L1_gnn_eb1': _L1_gnn_in['eb1'], 'L1_gnn_eW2': _L1_gnn_in['eW2'], 'L1_gnn_eb2': _L1_gnn_in['eb2'], 'L1_gnn_nW1': _L1_gnn_in['nW1'], 'L1_gnn_nb1': _L1_gnn_in['nb1'], 'L1_gnn_nW2': _L1_gnn_in['nW2'], 'L1_gnn_nb2': _L1_gnn_in['nb2'], 'L1_gnn_ln_gamma': _L1_gnn_in['ln_gamma'], 'L1_gnn_ln_beta': _L1_gnn_in['ln_beta']}

def reference(x, src, dst, edge_attr_64, edge_weight, L0_gnn_kernel, L0_gnn_bias, L1_gnn_eW1, L1_gnn_eb1, L1_gnn_eW2, L1_gnn_eb2, L1_gnn_nW1, L1_gnn_nb1, L1_gnn_nW2, L1_gnn_nb2, L1_gnn_ln_gamma, L1_gnn_ln_beta):
    import jax
    import jax.numpy as jnp

    def _L0_gnn_ref(x, edge_row, edge_col, edge_val, kernel, bias):
        import jax, jax.numpy as jnp
        import numpy as np
        N_NODES = 3125
        N_EDGES = 100000
        D_IN = 256
        UNITS = 256
        gathered = edge_val[:, None] * x[edge_col]
        agg = jax.ops.segment_sum(gathered, edge_row, num_segments=N_NODES)
        out = jnp.matmul(agg, kernel) + bias
        return jax.nn.relu(out)

    def _L1_gnn_ref(h, edge_index, edge_attr, eW1, eb1, eW2, eb2, nW1, nb1, nW2, nb2, ln_gamma, ln_beta):
        import jax, jax.numpy as jnp
        import numpy as np
        N_NODES = 50000
        N_EDGES = 15625
        HDIM = 256
        EDIM = 64
        MSG_H = 512
        UPD_H = 512
        LN_EPS = 1e-05

        def _mlp(x, W1, b1, W2, b2):
            return jax.nn.relu(x @ W1 + b1) @ W2 + b2

        def _layer_norm(x, gamma, beta):
            mu = jnp.mean(x, axis=-1, keepdims=True)
            var = jnp.mean(jnp.square(x - mu), axis=-1, keepdims=True)
            return (x - mu) * jax.lax.rsqrt(var + LN_EPS) * gamma + beta
        src = edge_index[0]
        dst = edge_index[1]
        m_in = jnp.concatenate([h[src], h[dst], edge_attr], axis=1)
        m = _mlp(m_in, eW1, eb1, eW2, eb2)
        agg = jax.ops.segment_sum(m, dst, num_segments=h.shape[0])
        h_upd = _mlp(jnp.concatenate([h, agg], axis=1), nW1, nb1, nW2, nb2)
        return _layer_norm(h + h_upd, ln_gamma, ln_beta)
    edge_index = jnp.stack([src, dst])
    x = _layernorm(x + _L0_gnn_ref(x, src, dst, edge_weight, L0_gnn_kernel, L0_gnn_bias), axis=-1)
    x = _layernorm(x + _L1_gnn_ref(x, edge_index, edge_attr_64, L1_gnn_eW1, L1_gnn_eb1, L1_gnn_eW2, L1_gnn_eb2, L1_gnn_nW1, L1_gnn_nb1, L1_gnn_nW2, L1_gnn_nb2, L1_gnn_ln_gamma, L1_gnn_ln_beta), axis=-1)
    return x

_drawn_inputs = setup_inputs


def setup_inputs(seed=0):
    import zlib

    import numpy as np

    out = dict(_drawn_inputs(seed))
    spreads = {'L0_gnn_bias': (0.0, 0.1),
     'L1_gnn_eb1': (0.0, 0.1),
     'L1_gnn_eb2': (0.0, 0.1),
     'L1_gnn_nb1': (0.0, 0.449),
     'L1_gnn_nb2': (0.0, 0.1),
     'L1_gnn_ln_gamma': (1.0, 0.2),
     'L1_gnn_ln_beta': (0.0, 0.1)}
    factors = {'edge_attr_64': 2.801}
    for name, (base, spread) in spreads.items():
        noise = np.random.default_rng([zlib.crc32(name.encode()), seed]).standard_normal(out[name].shape)
        drawn = base * np.exp(spread * noise) if base else spread * noise
        out[name] = jnp.asarray(drawn.astype(out[name].dtype))
    for name, factor in factors.items():
        out[name] = (out[name] * factor).astype(out[name].dtype)
    return out
```

```python
from contextlib import ExitStack

import concourse.bass as bass
from concourse import mybir

F32 = mybir.dt.float32
BF16 = mybir.dt.bfloat16
I32 = mybir.dt.int32
ALU = mybir.AluOpType
ACT = mybir.ActivationFunctionType
AX = mybir.AxisListType

P = 128
W = 64
TPI = 8
HT = TPI // 2
GPI = TPI // 2
TABLES = 4
D = 256
HID = 512
EA = 64
BPI = 5
NPI = BPI * P
EPS = 1e-5
FAR = 1 << 20


def build(nc, a, out, n_nodes, n_tiles):
    NG = n_tiles // 2
    NB = -(-n_nodes // NPI) * BPI
    NP = NB * P
    NK = NP // W
    NW = -(-n_nodes // W)
    TR = NP + P
    CP = NG // 2
    NI = NB // BPI

    xk_d = nc.dram_tensor("xk_scratch", (NP, D), F32, kind="Internal").ap()
    table = [nc.dram_tensor(f"table{r}_scratch", (TR, D), F32, kind="Internal").ap() for r in range(TABLES)]
    A_d = nc.dram_tensor("A_scratch", (NP, HID), F32, kind="Internal").ap()
    B_d = nc.dram_tensor("B_scratch", (NP, HID), F32, kind="Internal").ap()
    hn_d = nc.dram_tensor("h_scratch", (NP, D), F32, kind="Internal").ap()
    hT_d = nc.dram_tensor("hT_scratch", (D, NP), F32, kind="Internal").ap()
    deg_d = nc.dram_tensor("deg_scratch", (1, NP), F32, kind="Internal").ap()

    xk_f = xk_d.rearrange("n c -> (n c)")
    B_f = B_d.rearrange("n c -> (n c)")

    ctx = ExitStack()
    with ctx:
        def sb(c, name, shape, dt=F32):
            return c.enter_context(nc.sbuf_tensor(name, shape, dt))

        def pb(c, name, shape, dt=F32):
            return c.enter_context(nc.psum_tensor(name, shape, dt))

        def sem(name):
            return ctx.enter_context(nc.semaphore(name))

        def sems(name, n):
            return [sem(f"{name}{i}") for i in range(n)]

        def over_tiles(eng, body):
            body(0, True, False)
            with eng.Fori(1, n_tiles // TPI - 1) as i:
                body(eng.snap(i * TPI), False, False)
            body(n_tiles - TPI, False, True)

        def over_blocks(eng, body):
            body(0, True, False)
            with eng.Fori(1, NI - 1) as i:
                body(i, False, False)
            body(NI - 1, False, True)

        turn = sem("turn")

        def gate(eng):
            eng.sem_inc(turn, 1)

        def before(k, per, slots):
            q = k - 1
            while (q % per) % slots != k % slots:
                q -= 1
            return q + 1

        iota = sb(ctx, "iota", [P, W])
        iota64 = sb(ctx, "iota64", [P, W])
        pid = sb(ctx, "pid", [P, 1])
        pmod = sb(ctx, "pmod", [P, 1])
        ident = sb(ctx, "ident", [P, P])
        fold = sb(ctx, "fold", [P, W])
        tri = sb(ctx, "tri", [P, P])
        eps = sb(ctx, "eps", [P, 1])
        dst_c = sb(ctx, "dst_c", [P, n_tiles])
        src_c = sb(ctx, "src_c", [P, n_tiles])
        w_c = sb(ctx, "w_c", [P, n_tiles])
        spare_c = sb(ctx, "spare_c", [P, n_tiles])
        first_b = sb(ctx, "first_b", [P, NG])
        base = sb(ctx, "base", [P, NG])
        base_i = sb(ctx, "base_i", [P, NG], I32)
        col_i = sb(ctx, "col_i", [P, NG], I32)
        res_i = sb(ctx, "res_i", [P, NG], I32)
        res = sb(ctx, "res", [P, NG])
        col = sb(ctx, "col", [P, NG])
        many_i = sb(ctx, "many_i", [P, 1], I32)
        w2n = sb(ctx, "w2n", [P, 4, HID])
        b2n = sb(ctx, "b2n", [1, HID])

        s_iota = sem("s_iota")
        s_const = sem("s_const")
        s_chk = sem("s_chk")
        s_first = sem("s_first")
        s_dst = sem("s_dst")
        s_src = sem("s_src")
        s_w = sem("s_w")
        s_tables = sem("s_tables")
        s_bad = sem("s_bad")
        s_count = sem("s_count")
        s_zero = sem("s_zero")
        s_bias = sem("s_bias")

        st = ExitStack()
        with st:
            it_i = sb(st, "it_i", [P, P], I32)
            ip_i = sb(st, "ip_i", [P, 1], I32)
            im_i = sb(st, "im_i", [P, 1], I32)
            ones = sb(st, "ones", [P, P])
            dci = sb(st, "dci", [P, n_tiles], I32)
            sci = sb(st, "sci", [P, n_tiles], I32)
            chk = sb(st, "chk", [CP, 2, 2 * P], I32)
            real = sb(st, "real", [CP, 2, 2 * P])
            mn = sb(st, "mn", [CP, 2])
            mx = sb(st, "mx", [CP, 2])
            below = sb(st, "below", [CP, 2])
            last = sb(st, "last", [CP, 2])
            above = sb(st, "above", [CP, 2])
            either = sb(st, "either", [CP, 2])
            bad = sb(st, "bad", [CP, 1])
            first_i = sb(st, "first_i", [1, NG], I32)
            first = sb(st, "first", [1, NG])
            fast = sb(st, "fast", [P, 1])
            many = sb(st, "many", [P, 1])
            zero = sb(st, "zero", [P, D])
            bias = sb(st, "bias", [P, D])
            ps_b = pb(st, "ps_b", [P, 512])
            ps_c = pb(st, "ps_c", [P, 512])

            with nc.Block() as block:
                @block.sync
                def _(sp):
                    sp.dma_start(chk[:, :, :], a["dst_row"].rearrange("o (p g e) -> (o p) g e", g=2, e=2 * P)).then_inc(s_chk, 16)
                    sp.dma_start(first_i[:, :], a["dst_row"][:, 0:n_tiles * P:2 * P], allow_slow_non_contiguous=True).then_inc(s_first, 16)
                    sp.dma_start(dci[:, :], a["dst_col"]).then_inc(s_dst, 16)
                    sp.dma_start(sci[:, :], a["src_col"]).then_inc(s_src, 16)
                    sp.dma_start(w_c[:, :], a["w_col"]).then_inc(s_w, 16)
                    sp.wait_ge(s_w, 16)

                @block.scalar
                def _(act):
                    act.dma_start(bias[:, :], a["b0"].broadcast_to([P, D])).then_inc(s_bias, 16)
                    act.wait_ge(s_zero, 1)
                    act.wait_ge(s_bias, 16)
                    for r in range(TABLES):
                        fill = (zero if r else bias)[:, :]
                        act.dma_start(table[r].rearrange("(p n) c -> p n c", p=P),
                                      fill[:, None, :].broadcast_to([P, TR // P, D])).then_inc(s_tables, 16)
                    act.wait_ge(s_tables, 16 * TABLES)

                @block.gpsimd
                def _(pool):
                    pool.iota(it_i[:, :], [[1, P]], base=0, channel_multiplier=0).then_inc(s_iota, 1)
                    pool.iota(ip_i[:, :], [[0, 1]], base=0, channel_multiplier=1).then_inc(s_iota, 1)
                    pool.memset(zero[:, :], 0.0).then_inc(s_zero, 1)

                @block.tensor
                def _(pe):
                    pe.wait_ge(s_bad, 1)
                    pe.matmul(ps_c[:, 0:1], ones[0:CP, :], bad[:, :], start=True, stop=True).then_inc(s_count, 1)
                    pe.wait_ge(s_bad, 2)
                    pe.matmul(ps_b[:, 0:NG], ones[0:1, :], first[:, :], start=True, stop=True).then_inc(s_count, 1)

                @block.vector
                def _(dve):
                    done = [0]

                    def step(ins):
                        done[0] += 1
                        ins.then_inc(s_const, 1)
                        dve.wait_ge(s_const, done[0])

                    dve.memset(ones[:, :], 1.0)
                    dve.memset(eps[:, :], EPS)
                    dve.wait_ge(s_iota, 2)
                    dve.tensor_copy(iota[:, :], it_i[:, 0:W])
                    dve.tensor_copy(pid[:, :], ip_i[:, :])
                    step(dve.tensor_scalar(im_i[:, :], ip_i[:, :], W - 1, None, ALU.bitwise_and))
                    dve.tensor_scalar(iota64[:, :], iota[:, :], 1.0 / W, None, ALU.mult)
                    step(dve.tensor_copy(pmod[:, :], im_i[:, :]))
                    dve.tensor_scalar(ident[:, :], it_i[:, :], pid[:, :], None, ALU.is_equal)
                    dve.tensor_scalar(tri[:, :], it_i[:, :], pid[:, :], None, ALU.is_lt)
                    dve.tensor_scalar(fold[:, :], iota[:, :], pmod[:, :], None, ALU.is_equal)
                    dve.wait_ge(s_chk, 16)
                    dve.tensor_reduce(mn[:, :], chk[:, :, :], AX.X, ALU.min)
                    step(dve.scalar_tensor_tensor(real[:, :, :], chk[:, :, :], float(NP), chk[:, :, :], ALU.is_lt, ALU.mult))
                    dve.tensor_reduce(mx[:, :], real[:, :, :], AX.X, ALU.max)
                    step(dve.tensor_scalar(last[:, :], chk[:, :, 0], float(W - 1), None, ALU.add))
                    dve.tensor_tensor(below[:, :], mn[:, :], chk[:, :, 0], ALU.is_lt)
                    step(dve.tensor_tensor(above[:, :], mx[:, :], last[:, :], ALU.is_gt))
                    step(dve.tensor_tensor(either[:, :], below[:, :], above[:, :], ALU.add))
                    dve.tensor_reduce(bad[:, :], either[:, :], AX.X, ALU.add).then_inc(s_bad, 1)
                    dve.wait_ge(s_first, 16)
                    dve.tensor_copy(first[:, :], first_i[:, :]).then_inc(s_bad, 1)
                    dve.wait_ge(s_dst, 16)
                    dve.tensor_copy(dst_c[:, :], dci[:, :])
                    dve.wait_ge(s_src, 16)
                    step(dve.tensor_copy(src_c[:, :], sci[:, :]))
                    dve.tensor_scalar(spare_c[:, :], src_c[:, :], pid[:, :], -1.0, ALU.subtract, ALU.mult)
                    dve.wait_ge(s_count, 1)
                    dve.tensor_scalar(fast[:, :], ps_c[:, 0:1], 0.5, None, ALU.is_lt)
                    step(dve.tensor_scalar(many[:, :], ps_c[:, 0:1], 0.5, None, ALU.is_gt))
                    dve.tensor_copy(many_i[:, :], many[:, :])
                    dve.wait_ge(s_count, 2)
                    dve.tensor_scalar(first_b[:, :], ps_b[:, 0:NG], fast[:, :], None, ALU.mult)
                    step(dve.tensor_scalar(spare_c[:, :], spare_c[:, :], float(NP), None, ALU.add))

        s_kw = sem("s_kw")
        s_xt = sems("s_xt", BPI)
        s_xmm = sem("s_xmm")
        s_xcp = sem("s_xcp")
        s_xst = sems("s_xst", BPI)
        s_wt = sem("s_wt")
        s_lohi = sem("s_lohi")
        s_hot = sem("s_hot")
        s_hist = sem("s_hist")
        s_w2 = sem("s_w2")
        s_w2c = sem("s_w2c")
        s_degc = sem("s_degc")
        s_degt = sem("s_degt")
        s_degr = sem("s_degr")
        s_degst = sem("s_degst")

        st = ExitStack()
        with st:
            kw = sb(st, "kw", [P, 2, D])
            xt = sb(st, "xt", [P, BPI, 2, P])
            xo = sb(st, "xo", [P, BPI, D])
            w2t = sb(st, "w2t", [P, 2, HID])
            nwb = sb(st, "nwb", [P, 2, HID])
            b2c = sb(st, "b2c", [P, 2])
            di = sb(st, "di", [P, n_tiles], I32)
            lo_i = sb(st, "lo_i", [P, n_tiles], I32)
            hi_i = sb(st, "hi_i", [P, n_tiles], I32)
            lo = sb(st, "lo", [P, n_tiles])
            hi = sb(st, "hi", [P, n_tiles])
            lohot = sb(st, "lohot", [P, TPI, W], BF16)
            hihot = sb(st, "hihot", [P, TPI, NK], BF16)
            none = sb(st, "none", [P, W], BF16)
            degc = sb(st, "degc", [W, NK])
            degr = sb(st, "degr", [NK, W])
            ps_x = pb(st, "ps_x", [P, 2, 512])
            ps_d = pb(st, "ps_d", [P, 512])
            ps_t = pb(st, "ps_t", [P, 512])
            ps_w = pb(st, "ps_w", [P, 2, HID])
            ps_n = pb(st, "ps_n", [P, HID])

            with nc.Block() as block:
                @block.sync
                def _(sp):
                    xT = a["xT"].rearrange("(c p) n -> p c n", p=P)
                    sp.dma_start(kw[:, :, :], a["K"].rearrange("(c p) n -> p c n", p=P)).then_inc(s_kw, 16)

                    def body(i, start, end):
                        for s in range(BPI):
                            if not start:
                                sp.wait_ge(s_xmm, i * BPI + (s + 1 - BPI))
                            sp.dma_start(xt[:, s, :, :], xT[:, :, bass.ds(i * NPI + s * P, P)]).then_inc(s_xt[s], 16)

                    over_blocks(sp, body)
                    sp.wait_ge(s_degr, 1)
                    sp.dma_start(deg_d.rearrange("o (k r) -> (o k) r", r=W), degr[:, :]).then_inc(s_degst, 16)
                    sp.wait_ge(s_degst, 16)

                @block.gpsimd
                def _(pool):
                    pool.dma_start(w2t[:, :, :], a["eW2T"].rearrange("(c p) n -> p c n", p=P)).then_inc(s_wt, 16)
                    pool.dma_start(nwb[:, :, :], a["nW1"][D:2 * D, :].rearrange("(c p) n -> p c n", p=P)).then_inc(s_wt, 16)
                    pool.dma_start(b2c[:, :], a["eb2_col"]).then_inc(s_wt, 16)

                    def body(i, start, end):
                        for s in range(BPI):
                            pool.wait_ge(s_xcp, i * BPI + (s + 1))
                            pool.dma_start(xk_d[bass.ds(i * NPI + s * P, P), :], xo[:, s, :]).then_inc(s_xst[s], 16)

                    over_blocks(pool, body)
                    for s in range(BPI):
                        pool.wait_ge(s_xst[s], 16 * NI)

                @block.scalar
                def _(act):
                    def body(i, start, end):
                        for s in range(BPI):
                            act.wait_ge(s_xmm, i * BPI + (s + 1))
                            if not start:
                                act.wait_ge(s_xst[s], i * 16)
                            act.copy(xo[:, s, :], ps_x[:, s % 2, 0:D]).then_inc(s_xcp, 1)

                    over_blocks(act, body)
                    for c in range(4):
                        act.wait_ge(s_w2, c + 1)
                        act.copy(w2n[:, c, :], ps_w[:, c % 2, :]).then_inc(s_w2c, 1)
                    act.wait_ge(s_w2, 5)
                    act.copy(b2n[:, :], ps_n[0:1, :]).then_inc(s_w2c, 1)

                @block.tensor
                def _(pe):
                    pe.wait_ge(s_kw, 16)

                    def body(i, start, end):
                        for s in range(BPI):
                            pe.wait_ge(s_xt[s], i * 16 + 16)
                            if not start or s >= 2:
                                pe.wait_ge(s_xcp, i * BPI + before(s, BPI, 2))
                            for c in range(2):
                                mm = pe.matmul(ps_x[:, s % 2, 0:D], xt[:, s, c, :], kw[:, c, :], start=c == 0, stop=c == 1)
                            mm.then_inc(s_xmm, 1)

                    over_blocks(pe, body)
                    pe.wait_ge(s_wt, 48)
                    for c in range(4):
                        if c >= 2:
                            pe.wait_ge(s_w2c, c - 1)
                        for k in range(2):
                            mm = pe.matmul(ps_w[:, c % 2, :], w2t[:, k, c * P:(c + 1) * P], nwb[:, k, :], start=k == 0, stop=k == 1)
                        mm.then_inc(s_w2, 1)
                    for k in range(2):
                        mm = pe.matmul(ps_n[0:1, :], b2c[:, k:k + 1], nwb[:, k, :], start=k == 0, stop=k == 1)
                    mm.then_inc(s_w2, 1)
                    pe.wait_ge(s_lohi, 1)
                    pe.matmul(ps_d[0:W, 0:NK], none[:, :], none[:, 0:1].broadcast_to([P, NK]), start=True, stop=False)

                    def counts(t, start, end):
                        for j in range(TPI):
                            if j % HT == 0:
                                pe.wait_ge(s_hot, t + j + HT)
                            mm = pe.matmul(ps_d[0:W, 0:NK], lohot[:, j, :], hihot[:, j, :], start=False, stop=False)
                            mm.then_inc(s_hist, 1)

                    over_tiles(pe, counts)
                    pe.matmul(ps_d[0:W, 0:NK], none[:, :], none[:, 0:1].broadcast_to([P, NK]), start=False, stop=True).then_inc(s_hist, 1)
                    pe.wait_ge(s_degc, 1)
                    pe.transpose(ps_t[0:NK, 0:W], degc[:, :], ident[0:W, 0:W]).then_inc(s_degt, 1)

                @block.vector
                def _(dve):
                    seq = [1]

                    def step(ins):
                        seq[0] += 1
                        ins.then_inc(s_lohi, 1)
                        dve.wait_ge(s_lohi, seq[0])

                    dve.memset(none[:, :], 0.0).then_inc(s_lohi, 1)
                    step(dve.tensor_copy(di[:, :], dst_c[:, :]))
                    dve.tensor_scalar(lo_i[:, :], di[:, :], W - 1, None, ALU.bitwise_and)
                    step(dve.tensor_scalar(hi_i[:, :], di[:, :], 6, None, ALU.arith_shift_right))
                    dve.tensor_copy(lo[:, :], lo_i[:, :])
                    step(dve.tensor_copy(hi[:, :], hi_i[:, :]))

                    def body(t, start, end):
                        for hh in range(2):
                            if not start:
                                dve.wait_ge(s_hist, t + HT * hh - HT)
                            j = slice(HT * hh, HT * hh + HT)
                            at = bass.ds(t + HT * hh, HT)
                            dve.tensor_tensor(lohot[:, j, :], iota[:, None, 0:W].broadcast_to([P, HT, W]),
                                              lo[:, at][:, :, None].broadcast_to([P, HT, W]), ALU.is_equal)
                            dve.tensor_tensor(hihot[:, j, :], iota[:, None, 0:NK].broadcast_to([P, HT, NK]),
                                              hi[:, at][:, :, None].broadcast_to([P, HT, NK]), ALU.is_equal).then_inc(s_hot, HT)

                    over_tiles(dve, body)
                    dve.wait_ge(s_hist, n_tiles + 1)
                    dve.tensor_copy(degc[:, :], ps_d[0:W, 0:NK]).then_inc(s_degc, 1)
                    dve.wait_ge(s_degt, 1)
                    dve.tensor_copy(degr[:, :], ps_t[0:NK, 0:W]).then_inc(s_degr, 1)

        def window_tables(dve, s_tab, first_pass, more):
            seq = [0]

            def step(ins):
                seq[0] += 1
                ins.then_inc(s_tab, 1)
                dve.wait_ge(s_tab, seq[0])

            if first_pass:
                step(dve.tensor_copy(base[:, :], first_b[:, :]))
            else:
                step(dve.tensor_scalar(base[:, :], base[:, :], float(W), None, ALU.add))
            step(dve.tensor_copy(base_i[:, :], base[:, :]))
            dve.tensor_scalar(col_i[:, :], base_i[:, :], 6, None, ALU.arith_shift_right)
            step(dve.tensor_scalar(res_i[:, :], base_i[:, :], W - 1, None, ALU.bitwise_and))
            step(dve.tensor_copy(res[:, :], res_i[:, :]))
            step(dve.tensor_tensor(col[:, :], base[:, :], res[:, :], ALU.subtract))
            more(step)
            return seq[0]

        c_tab = sem("c_tab")
        c_srow = sems("c_srow", 2)
        c_win = sems("c_win", GPI)
        c_hot = sem("c_hot")
        c_pick = sem("c_pick")
        c_pickc = sem("c_pickc")
        c_msg = sem("c_msg")
        c_msgc = sem("c_msgc")
        c_dup = sem("c_dup")
        c_idx = sem("c_idx")
        c_add = sems("c_add", TPI)

        def neighbour_sum(first_pass):
            st = ExitStack()
            with st:
                tag = "a" if first_pass else "b"
                srow = sb(st, "srow_n" + tag, [P, TPI, P], I32)
                win = sb(st, "win_n" + tag, [W, GPI, D])
                rel = sb(st, "rel_n" + tag, [P, n_tiles])
                whot = sb(st, "whot_n" + tag, [P, TPI, W])
                same = sb(st, "same_n" + tag, [P, TPI, P])
                junk = sb(st, "junk_n" + tag, [P, TPI, P])
                dup = sb(st, "dup_n" + tag, [P, TPI])
                jump = sb(st, "jump_n" + tag, [P, TPI])
                idx = sb(st, "idx_n" + tag, [P, TPI], I32)
                pick = sb(st, "pick_n" + tag, [W, TPI, P])
                msg = sb(st, "msg_n" + tag, [P, TPI, D])
                ps_p = pb(st, "ps_p_n" + tag, [W, 2, HT * P])
                ps_m = pb(st, "ps_m_n" + tag, [P, TPI // 2, 2 * D])
                NTAB = 7

                with nc.Block() as block:
                    @block.sync
                    def _(sp):
                        sp.wait_ge(c_tab, NTAB)

                        def body(t, start, end):
                            for hh in range(2):
                                if not start:
                                    sp.wait_ge(c_dup, t + HT * hh + HT - TPI)
                                sp.dma_start(srow[:, HT * hh:HT * hh + HT, :],
                                             a["src_row"][:, bass.ds(t * P + HT * hh * P, HT * P)]
                                             .rearrange("o (j e) -> o j e", e=P).broadcast_to([P, HT, P])).then_inc(c_srow[hh], 16)
                                for g in (2 * hh, 2 * hh + 1):
                                    at = sp.snap(sp.value_load(base_i[0:1, bass.ds(t // 2 + g, 1)], min_val=0, max_val=NP - W) * D)
                                    if not start:
                                        sp.wait_ge(c_msg, t + 2 * g + 2 - TPI)
                                    sp.dma_start(win[:, g, :], xk_f[bass.ds(at, W * D)].rearrange("(n c) -> n c", c=D)).then_inc(c_win[g], 16)

                        over_tiles(sp, body)

                    @block.vector
                    def _(dve):
                        def more(step):
                            step(dve.tensor_tensor(rel[:, :].rearrange("p (g j) -> p g j", j=2),
                                                   dst_c[:, :].rearrange("p (g j) -> p g j", j=2),
                                                   base[:, :, None].broadcast_to([P, NG, 2]), ALU.subtract))

                        n = window_tables(dve, c_tab, first_pass, more)
                        dve.sem_inc(c_tab, NTAB - n)

                        def body(t, start, end):
                            for hh in range(2):
                                dve.wait_ge(c_srow[hh], t * 2 + 16)
                                for j in range(HT * hh, HT * hh + HT):
                                    at = bass.ds(t + j, 1)
                                    if not start:
                                        dve.wait_ge(c_pick, t + j + 1 - TPI)
                                    dve.tensor_scalar(whot[:, j, :], iota[:, :], rel[:, at], w_c[:, at], ALU.is_equal, ALU.mult)
                                    dve.tensor_scalar(same[:, j, :], srow[:, j, :], src_c[:, at], None,
                                                      ALU.is_equal).then_inc(c_hot, 1)
                                    dve.scalar_tensor_tensor(junk[:, j, :], srow[:, j, :], src_c[:, at], tri[:, :], ALU.is_equal,
                                                             ALU.mult, accum_out=dup[:, j:j + 1]).then_inc(c_dup, 1)
                                js = slice(HT * hh, HT * hh + HT)
                                cols = bass.ds(t + HT * hh, HT)
                                dve.wait_ge(c_dup, t + HT * hh + HT)
                                dve.scalar_tensor_tensor(jump[:, js], dup[:, js], 1.0, spare_c[:, cols], ALU.min,
                                                         ALU.mult).then_inc(c_tab, 1)
                                dve.wait_ge(c_tab, jumps(t, hh))
                                if not start:
                                    for j in range(HT * hh, HT * hh + HT):
                                        dve.wait_ge(c_add[j], t * 2)
                                dve.tensor_tensor(idx[:, js], jump[:, js], src_c[:, cols], ALU.add).then_inc(c_idx, HT)

                        def jumps(t, hh):
                            return t // HT + (NTAB + hh + 1)

                        over_tiles(dve, body)

                    @block.tensor
                    def _(pe):
                        def body(t, start, end):
                            for hh in range(2):
                                if not start:
                                    pe.wait_ge(c_pickc, t + HT * hh + HT - TPI)
                                for j in range(HT * hh, HT * hh + HT):
                                    pe.wait_ge(c_hot, t + j + 1)
                                    pe.matmul(ps_p[:, hh, (j % HT) * P:(j % HT + 1) * P], whot[:, j, :], same[:, j, :],
                                              start=True, stop=True).then_inc(c_pick, 1)
                                pe.wait_ge(c_pickc, t + HT * hh + HT)
                                for j in range(HT * hh, HT * hh + HT):
                                    if j % 2 == 0:
                                        pe.wait_ge(c_win[j // 2], t * 2 + 16)
                                        if not start:
                                            pe.wait_ge(c_msgc, t + j + 2 - TPI)
                                    pe.matmul(ps_m[:, j // 2, (j % 2) * D:(j % 2 + 1) * D], pick[:, j, :], win[:, j // 2, :],
                                              start=True, stop=True).then_inc(c_msg, 1)

                        over_tiles(pe, body)

                    @block.scalar
                    def _(act):
                        def body(t, start, end):
                            for hh in range(2):
                                act.wait_ge(c_pick, t + HT * hh + HT)
                                if not start:
                                    act.wait_ge(c_msg, t + HT * hh + HT - TPI)
                                act.copy(pick[:, HT * hh:HT * hh + HT, :],
                                         ps_p[:, hh, :].rearrange("p (j e) -> p j e", e=P)).then_inc(c_pickc, HT)
                                for q in (2 * hh, 2 * hh + 1):
                                    act.wait_ge(c_msg, t + 2 * q + 2)
                                    if not start:
                                        for j in (2 * q, 2 * q + 1):
                                            act.wait_ge(c_add[j], t * 2)
                                    act.copy(msg[:, 2 * q:2 * q + 2, :],
                                             ps_m[:, q, :].rearrange("p (j c) -> p j c", c=D)).then_inc(c_msgc, 2)

                        over_tiles(act, body)

                    @block.gpsimd
                    def _(pool):
                        def body(t, start, end):
                            for j in range(TPI):
                                if j % 2 == 0:
                                    pool.wait_ge(c_msgc, t + j + 2)
                                if j % HT == 0:
                                    pool.wait_ge(c_idx, t + j + HT)
                                if j >= TABLES:
                                    pool.wait_ge(c_add[j - TABLES], t * 2 + 16)
                                elif not start:
                                    pool.wait_ge(c_add[j - TABLES + TPI], t * 2)
                                gate(pool)
                                pool.indirect_dma_start(table[j % TABLES][:, :], bass.IndirectOffsetOnAxis(ap=idx[:, j:j + 1], axis=0),
                                                        msg[:, j, :], None, compute_op=ALU.add).then_inc(c_add[j], 16)

                        over_tiles(pool, body)
                        for j in range(TPI):
                            pool.wait_ge(c_add[j], 2 * n_tiles)

        pass_sems = [c_tab, *c_srow, *c_win, c_hot, c_pick, c_pickc, c_msg, c_msgc, c_dup, c_idx, *c_add]

        def clear(which):
            numbers = range(min(s.num for s in which), max(s.num for s in which) + 1)
            with nc.Block() as block:
                @block.gpsimd
                def _(pool):
                    pool.dma_reset(numbers)

                @block.sync
                def _(sp):
                    sp.drain(semaphore_range=numbers)
            with nc.Block() as block:
                @block.gpsimd
                def _(pool):
                    pool.sem_clear(numbers)

        def over_windows(one_pass, which):
            one_pass(True)
            again = nc.values_load(many_i[0:1, 0:1], min_val=0, max_val=1)
            with nc.If(again > 0):
                with nc.Fori(1, NW) as _w:
                    clear(which)
                    one_pass(False)

        over_windows(neighbour_sum, pass_sems)

        n_w = sem("n_w")
        n_half = sem("n_half")
        n_in = sem("n_in")
        n_sum = sem("n_sum")
        n_var = sem("n_var")
        n_rs = sem("n_rs")
        n_h = sem("n_h")
        n_t = sem("n_t")
        n_tc = sem("n_tc")
        n_ab = sem("n_ab")
        n_abc = sem("n_abc")
        n_b = sem("n_b")
        n_st = sems("n_st", BPI)

        st = ExitStack()
        with st:
            wa = sb(st, "wa", [P, 2, HID])
            wb = sb(st, "wb", [P, 2, HID])
            eb1 = sb(st, "eb1", [P, HID])
            half = sb(st, "half", [P, BPI])
            part = sb(st, "part", [P, TABLES, BPI, D])
            xin = sb(st, "xin", [P, BPI, D])
            pair0 = sb(st, "pair0", [P, BPI, D])
            pair1 = sb(st, "pair1", [P, BPI, D])
            both = sb(st, "both", [P, BPI, D])
            pre = sb(st, "pre", [P, BPI, D])
            stats = sb(st, "stats", [P, BPI, 6])
            mv = sb(st, "mv", [P, BPI, 2])
            vare = sb(st, "vare", [P, BPI])
            rstd = sb(st, "rstd", [P, BPI])
            h = sb(st, "h", [P, BPI, D])
            hT = sb(st, "hT", [P, BPI, 2, P])
            ao = sb(st, "ao", [P, BPI, HID])
            bo = sb(st, "bo", [P, BPI, HID])
            bb = sb(st, "bb", [P, BPI, HID])
            ps_t = pb(st, "ps_th", [P, 2, 512])
            ps_ab = pb(st, "ps_ab", [P, 4, HID])

            with nc.Block() as block:
                @block.gpsimd
                def _(pool):
                    pool.memset(half[:, :], -0.5).then_inc(n_half, 1)

                    def load(i):
                        for r in range(TABLES):
                            pool.dma_start(part[:, r, :, :], table[r][bass.ds(i * NPI, NPI), :].rearrange("(s p) c -> p s c", p=P)).then_inc(n_in, 16)
                        pool.dma_start(xin[:, :, :], a["x"][bass.ds(i * NPI, NPI), :].rearrange("(s p) c -> p s c", p=P)).then_inc(n_in, 16)

                    load(0)
                    pool.wait_ge(n_half, 1)

                    def body(i, start, end):
                        pool.wait_ge(n_var, i + 1)
                        pool.tensor_tensor(rstd[:, :], vare[:, :], half[:, :], ALU.pow).then_inc(n_rs, 1)
                        if not end:
                            load(i + 1)
                        if start:
                            pool.wait_ge(n_w, 48)
                        for s in range(BPI):
                            pool.wait_ge(n_abc, i * (2 * BPI) + (2 * s + 2))
                            if not start:
                                pool.wait_ge(n_st[s], i * 64)
                            pool.tensor_tensor(bb[:, s, :], bo[:, s, :], eb1[:, :], ALU.add).then_inc(n_b, 1)

                    over_blocks(pool, body)

                @block.vector
                def _(dve):
                    def body(i, start, end):
                        dve.wait_ge(n_in, i * (16 * (TABLES + 1)) + 16 * (TABLES + 1))
                        dve.tensor_tensor(pair0[:, :, :], part[:, 0, :, :], part[:, 1, :, :], ALU.add)
                        dve.tensor_tensor(pair1[:, :, :], part[:, 2, :, :], part[:, 3, :, :], ALU.add).then_inc(n_sum, 1)
                        dve.wait_ge(n_sum, i * 5 + 1)
                        dve.tensor_tensor(both[:, :, :], pair0[:, :, :], pair1[:, :, :], ALU.add).then_inc(n_sum, 1)
                        dve.wait_ge(n_sum, i * 5 + 2)
                        dve.scalar_tensor_tensor(pre[:, :, :], both[:, :, :], 0.0, xin[:, :, :], ALU.max, ALU.add).then_inc(n_sum, 1)
                        dve.wait_ge(n_sum, i * 5 + 3)
                        for s in range(BPI):
                            ins = dve.bn_stats(stats[:, s, :], pre[:, s, :])
                        ins.then_inc(n_sum, 1)
                        dve.wait_ge(n_sum, i * 5 + 4)
                        gate(dve)
                        for s in range(BPI):
                            ins = dve.bn_aggr(mv[:, s, :], stats[:, s, :])
                        ins.then_inc(n_sum, 1)
                        dve.wait_ge(n_sum, i * 5 + 5)
                        dve.tensor_scalar(vare[:, :], mv[:, :, 1], EPS, None, ALU.add).then_inc(n_var, 1)
                        dve.wait_ge(n_rs, i + 1)
                        for s in range(BPI):
                            if not start:
                                dve.wait_ge(n_t, i * BPI + (s + 1 - BPI))
                                dve.wait_ge(n_st[s], i * 64)
                            dve.tensor_scalar(h[:, s, :], pre[:, s, :], mv[:, s, 0:1], rstd[:, s:s + 1], ALU.subtract,
                                              ALU.mult).then_inc(n_h, 1)

                    over_blocks(dve, body)

                @block.tensor
                def _(pe):
                    pe.wait_ge(n_w, 48)

                    def body(i, start, end):
                        for s in range(BPI):
                            pe.wait_ge(n_h, i * BPI + (s + 1))
                            if not start or s >= 2:
                                pe.wait_ge(n_tc, i * BPI + before(s, BPI, 2))
                            for c in range(2):
                                mm = pe.transpose(ps_t[:, s % 2, c * P:(c + 1) * P], h[:, s, c * P:(c + 1) * P], ident[:, :])
                            mm.then_inc(n_t, 1)
                            pe.wait_ge(n_tc, i * BPI + (s + 1))
                            for z, w in enumerate((wa, wb)):
                                slot = (2 * s + z) % 4
                                if not start or s >= 2:
                                    pe.wait_ge(n_abc, i * (2 * BPI) + before(2 * s + z, 2 * BPI, 4))
                                for c in range(2):
                                    mm = pe.matmul(ps_ab[:, slot, :], hT[:, s, c, :], w[:, c, :], start=c == 0, stop=c == 1)
                                mm.then_inc(n_ab, 1)

                    over_blocks(pe, body)

                @block.scalar
                def _(act):
                    act.dma_start(wa[:, :, :], a["eW1"][0:D, :].rearrange("(c p) n -> p c n", p=P)).then_inc(n_w, 16)
                    act.dma_start(wb[:, :, :], a["eW1"][D:2 * D, :].rearrange("(c p) n -> p c n", p=P)).then_inc(n_w, 16)
                    act.dma_start(eb1[:, :], a["eb1"].broadcast_to([P, HID])).then_inc(n_w, 16)

                    def body(i, start, end):
                        for s in range(BPI):
                            act.wait_ge(n_t, i * BPI + (s + 1))
                            if not start:
                                act.wait_ge(n_ab, i * (2 * BPI) + (2 * s + 2 - 2 * BPI))
                                act.wait_ge(n_st[s], i * 64)
                            act.copy(hT[:, s, :, :], ps_t[:, s % 2, 0:2 * P].rearrange("p (c n) -> p c n", c=2)).then_inc(n_tc, 1)
                            for z in range(2):
                                act.wait_ge(n_ab, i * (2 * BPI) + (2 * s + z + 1))
                                if z and not start:
                                    act.wait_ge(n_b, i * BPI + (s + 1 - BPI))
                                act.copy((bo if z else ao)[:, s, :], ps_ab[:, (2 * s + z) % 4, :]).then_inc(n_abc, 1)

                    over_blocks(act, body)

                @block.sync
                def _(sp):
                    hT_v = hT_d.rearrange("(c p) n -> p c n", p=P)

                    def body(i, start, end):
                        for s in range(BPI):
                            rows = bass.ds(i * NPI + s * P, P)
                            sp.wait_ge(n_tc, i * BPI + (s + 1))
                            sp.dma_start(hT_v[:, :, rows], hT[:, s, :, :]).then_inc(n_st[s], 16)
                            sp.wait_ge(n_h, i * BPI + (s + 1))
                            sp.dma_start(hn_d[rows, :], h[:, s, :]).then_inc(n_st[s], 16)
                            sp.wait_ge(n_abc, i * (2 * BPI) + (2 * s + 1))
                            sp.dma_start(A_d[rows, :], ao[:, s, :]).then_inc(n_st[s], 16)
                            sp.wait_ge(n_b, i * BPI + (s + 1))
                            sp.dma_start(B_d[rows, :], bb[:, s, :]).then_inc(n_st[s], 16)

                    over_blocks(sp, body)
                    for s in range(BPI):
                        sp.wait_ge(n_st[s], 64 * NI)

        S = sb(ctx, "S", [P, NK, HID])
        m_zero = sem("m_zero")
        m_tab = sem("m_tab")
        m_wc = sem("m_wc")
        m_ea = sems("m_ea", 2)
        m_drow = sems("m_drow", 2)
        m_idx = sems("m_idx", 2)
        m_win = sems("m_win", GPI)
        m_gat = sems("m_gat", TPI)
        m_row = sem("m_row")
        m_hot = sem("m_hot")
        m_pre = sem("m_pre")
        m_add = sem("m_add")
        m_relu = sem("m_relu")
        m_agg = sem("m_agg")
        m_out = sem("m_out")

        with nc.Block() as block:
            @block.gpsimd
            def _(pool):
                pool.memset(S[:, 0:NK // 2, :], 0.0).then_inc(m_zero, 1)

            @block.vector
            def _(dve):
                dve.memset(S[:, NK // 2:NK, :], 0.0).then_inc(m_zero, 1)

        def message_sum(first_pass):
            st = ExitStack()
            with st:
                tag = "a" if first_pass else "b"
                lhs = sb(st, "lhs_m" + tag, [P, TPI, P])
                rhs = sb(st, "rhs_m" + tag, [P, GPI, HID])
                drow = sb(st, "drow_m" + tag, [W, TPI, P], I32)
                gidx = sb(st, "gidx_m" + tag, [P, TPI], I32)
                winid = sb(st, "winid_m" + tag, [P, NG])
                rel = sb(st, "rel_m" + tag, [P, n_tiles])
                below = sb(st, "below_m" + tag, [P, NG])
                above = sb(st, "above_m" + tag, [P, NG])
                wrow = sb(st, "wrow_m" + tag, [P, GPI, W])
                hot = sb(st, "hot_m" + tag, [P, TPI, W])
                gat = sb(st, "gat_m" + tag, [P, TPI, HID])
                pre = sb(st, "pre_m" + tag, [P, HT, HID])
                hid = sb(st, "hid_m" + tag, [P, TPI, HID])
                ps_p = pb(st, "ps_p_m" + tag, [P, HT, HID])
                ps_a = pb(st, "ps_a_m" + tag, [P, GPI, HID])
                NTAB = 8 + 3

                with nc.Block() as block:
                    @block.sync
                    def _(sp):
                        for g in range(GPI):
                            sp.dma_start(rhs[W:P, g, :], a["eW1"][2 * D:2 * D + EA, :]).then_inc(m_wc, 16)
                        sp.wait_ge(m_tab, 3)

                        def body(t, start, end):
                            for hh in range(2):
                                js = slice(HT * hh, HT * hh + HT)
                                edges = bass.ds(t * P + HT * hh * P, HT * P)
                                if not start:
                                    for j in range(HT * hh, HT * hh + HT):
                                        sp.wait_ge(m_gat[j], t * 2)
                                    gate(sp)
                                sp.dma_start(gidx[:, js], a["src_col"][:, bass.ds(t + HT * hh, HT)]).then_inc(m_idx[hh], 16)
                                if not start:
                                    sp.wait_ge(m_hot, t + HT * hh + HT - TPI)
                                sp.dma_start(drow[:, js, :], a["dst_row"][:, edges].rearrange("o (j e) -> o j e", e=P)
                                             .broadcast_to([W, HT, P])).then_inc(m_drow[hh], 16)
                                at = [sp.snap(sp.value_load(base_i[0:1, bass.ds(t // 2 + g, 1)], min_val=0, max_val=NP - W) * HID)
                                      for g in (2 * hh, 2 * hh + 1)]
                                if not start:
                                    sp.wait_ge(m_pre, t + HT * hh + HT - TPI)
                                sp.dma_start(lhs[W:P, js, :], a["eaT"][:, edges].rearrange("f (j e) -> f j e", e=P)).then_inc(m_ea[hh], 16)
                                for g in (2 * hh, 2 * hh + 1):
                                    sp.dma_start(rhs[0:W, g, :], B_f[bass.ds(at[g % 2], W * HID)].rearrange("(n c) -> n c", c=HID)
                                                 ).then_inc(m_win[g], 16)

                        over_tiles(sp, body)

                    @block.gpsimd
                    def _(pool):
                        def body(t, start, end):
                            for j in range(TPI):
                                if j % HT == 0:
                                    pool.wait_ge(m_idx[j // HT], t * 2 + 16)
                                if not start:
                                    pool.wait_ge(m_add, t + j + 1 - TPI)
                                gate(pool)
                                pool.indirect_dma_start(gat[:, j, :], None, A_d[:, :],
                                                        bass.IndirectOffsetOnAxis(ap=gidx[:, j:j + 1], axis=0)).then_inc(m_gat[j], 16)

                        over_tiles(pool, body)

                    @block.vector
                    def _(dve):
                        def more(step):
                            step(dve.tensor_scalar(winid[:, :], base[:, :], pid[:, :], None, ALU.add))
                            step(dve.tensor_tensor(rel[:, :].rearrange("p (g j) -> p g j", j=2),
                                                   dst_c[:, :].rearrange("p (g j) -> p g j", j=2),
                                                   col[:, :, None].broadcast_to([P, NG, 2]), ALU.subtract))
                            step(dve.tensor_scalar(rel[:, :], rel[:, :], 1.0 / W, None, ALU.mult))
                            step(dve.tensor_scalar(above[:, :], res[:, :], pmod[:, :], None, ALU.is_le))
                            step(dve.tensor_scalar(below[:, :], res[:, :], pmod[:, :], None, ALU.is_gt))

                        window_tables(dve, m_tab, first_pass, more)

                        def hots(t, g, start):
                            tile = t + 2 * g
                            grp = bass.ds(t // 2 + g, 1)
                            if g % 2 == 0:
                                dve.wait_ge(m_drow[g // 2], t * 2 + 16)
                            if not start:
                                dve.wait_ge(m_pre, tile + 2 - TPI)
                                dve.wait_ge(m_agg, tile + 2 - TPI)
                            dve.tensor_scalar(lhs[0:W, 2 * g:2 * g + 2, :], drow[:, 2 * g:2 * g + 2, :], winid[0:W, grp], None,
                                              ALU.is_equal)
                            dve.scalar_tensor_tensor(wrow[:, g, :], iota[:, :], res[:, grp], iota64[:, :], ALU.is_lt,
                                                     ALU.add).then_inc(m_row, 1)
                            dve.wait_ge(m_row, t // 2 + (g + 1))
                            for j in (2 * g, 2 * g + 1):
                                dve.tensor_scalar(hot[:, j, :], wrow[:, g, :], rel[:, bass.ds(t + j, 1)], None,
                                                  ALU.is_equal).then_inc(m_hot, 1)

                        def add_a(t, g, start):
                            for j in (2 * g, 2 * g + 1):
                                dve.wait_ge(m_gat[j], t * 2 + 16)
                                dve.wait_ge(m_pre, t + j + 1)
                                if not start or j >= HT:
                                    dve.wait_ge(m_relu, t + j + 1 - HT)
                                dve.tensor_tensor(pre[:, j % HT, :], ps_p[:, j % HT, :], gat[:, j, :], ALU.add).then_inc(m_add, 1)

                        def to_s(t, g, start):
                            at = dve.value_load(col_i[0:1, bass.ds(t // 2 + g, 1)], min_val=0, max_val=NK - 2)
                            grp = bass.ds(t // 2 + g, 1)
                            dve.wait_ge(m_agg, t + 2 * g + 2)
                            if not start or g:
                                dve.wait_ge(m_out, t + 2 * g)
                            dve.scalar_tensor_tensor(S[:, bass.ds(at, 1), :], ps_a[:, g:g + 1, :], above[:, grp],
                                                     S[:, bass.ds(at, 1), :], ALU.mult, ALU.add).then_inc(m_out, 1)
                            dve.scalar_tensor_tensor(S[:, bass.ds(at + 1, 1), :], ps_a[:, g:g + 1, :], below[:, grp],
                                                     S[:, bass.ds(at + 1, 1), :], ALU.mult, ALU.add).then_inc(m_out, 1)

                        hots(0, 0, True)
                        hots(0, 1, True)

                        def body(t, start, end):
                            for g in range(GPI):
                                if g < 2:
                                    hots(t, g + 2, start)
                                elif not end:
                                    hots(t + TPI, g - 2, False)
                                add_a(t, g, start)
                                if g:
                                    to_s(t, g - 1, start)
                                elif not start:
                                    to_s(t - TPI, GPI - 1, False)

                        over_tiles(dve, body)
                        to_s(n_tiles - TPI, GPI - 1, False)

                    @block.scalar
                    def _(act):
                        def body(t, start, end):
                            for j in range(TPI):
                                act.wait_ge(m_add, t + j + 1)
                                if not start:
                                    act.wait_ge(m_agg, t + j + 1 - TPI)
                                act.activation(hid[:, j, :], pre[:, j % HT, :], ACT.Relu).then_inc(m_relu, 1)

                        over_tiles(act, body)

                    @block.tensor
                    def _(pe):
                        pe.wait_ge(m_wc, 16 * GPI)

                        def products(t, g, start):
                            if g % 2 == 0:
                                pe.wait_ge(m_ea[g // 2], t * 2 + 16)
                            pe.wait_ge(m_win[g], t * 2 + 16)
                            pe.wait_ge(m_hot, t + 2 * g + 2)
                            for j in (2 * g, 2 * g + 1):
                                if not start or j >= HT:
                                    pe.wait_ge(m_add, t + j + 1 - HT)
                                pe.matmul(ps_p[:, j % HT, :], lhs[:, j, :], rhs[:, g, :], start=True, stop=True).then_inc(m_pre, 1)

                        def sums(t, g, start):
                            if not start:
                                pe.wait_ge(m_out, t + 2 * g + 2 - TPI)
                            for j in (2 * g, 2 * g + 1):
                                pe.wait_ge(m_relu, t + j + 1)
                                q = W * (j % 2)
                                pe.matmul(ps_a[q:q + W, g, :], hot[:, j, :], hid[:, j, :], start=True, stop=True).then_inc(m_agg, 1)

                        products(0, 0, True)
                        products(0, 1, True)

                        def body(t, start, end):
                            for g in range(GPI):
                                if g < 2:
                                    products(t, g + 2, start)
                                elif not end:
                                    products(t + TPI, g - 2, False)
                                sums(t, g, start)

                        over_tiles(pe, body)

        over_windows(message_sum, [m_tab, m_wc, *m_ea, *m_drow, *m_idx, *m_win, *m_gat, m_row, m_hot, m_pre, m_add,
                                   m_relu, m_agg, m_out])

        f_w = sem("f_w")
        f_gb = sem("f_gb")
        f_half = sem("f_half")
        f_s = sem("f_s")
        f_h = sem("f_h")
        f_hin = sem("f_hin")
        f_hb = sem("f_hb")
        f_t = sem("f_t")
        f_tc = sem("f_tc")
        f_z = sem("f_z")
        f_u = sem("f_u")
        f_o = sem("f_o")
        f_y = sem("f_y")
        f_seq = sem("f_seq")
        f_var = sem("f_var")
        f_rs = sem("f_rs")
        f_n = sem("f_n")
        f_g = sem("f_g")
        f_out = sem("f_out")
        f_st = sem("f_st")
        NV = NPI // 2
        KV = NV // W

        st = ExitStack()
        with st:
            nwa = sb(st, "nwa", [P, 2, HID])
            nw2 = sb(st, "nw2", [P, 4, D])
            nb1 = sb(st, "nb1", [P, 4])
            gam = sb(st, "gam", [P, D])
            bet = sb(st, "bet", [P, D])
            half = sb(st, "half2", [P, BPI])
            sst = sb(st, "sst", [P, 2 * KV, HID])
            hT = sb(st, "hT2", [P, 2, NPI])
            deg = sb(st, "deg2", [1, NPI])
            nb2 = sb(st, "nb2", [P, D])
            hin = sb(st, "hin", [P, BPI, D])
            hb = sb(st, "hb", [P, BPI, D])
            hbeta = sb(st, "hbeta", [P, BPI, D])
            sT = sb(st, "sT", [P, 2, 4, NV])
            uT = sb(st, "uT", [P, 4, NPI])
            y = sb(st, "y", [P, BPI, D])
            y2 = sb(st, "y2", [P, BPI, D])
            stats = sb(st, "stats2", [P, BPI, 6])
            mv = sb(st, "mv2", [P, BPI, 2])
            vare = sb(st, "vare2", [P, BPI])
            rstd = sb(st, "rstd2", [P, BPI])
            ps_s = pb(st, "ps_s", [P, 2, 512])
            ps_z = pb(st, "ps_z", [P, 2, 512])
            ps_o = pb(st, "ps_o", [P, 2, 512])

            with nc.Block() as block:
                @block.sync
                def _(sp):
                    sp.dma_start(nwa[:, :, :], a["nW1"][0:D, :].rearrange("(c p) n -> p c n", p=P)).then_inc(f_w, 16)
                    sp.dma_start(nw2[:, :, :], a["nW2"].rearrange("(c p) n -> p c n", p=P)).then_inc(f_w, 16)
                    sp.dma_start(nb1[:, :], a["nb1_col"]).then_inc(f_w, 16)
                    hT_v = hT_d.rearrange("(c p) n -> p c n", p=P)

                    def body(i, start, end):
                        if not start:
                            sp.wait_ge(f_t, i * 8)
                        sp.dma_start(sst[:, :, :], S[:, bass.ds(i * (2 * KV), 2 * KV), :]).then_inc(f_s, 16)
                        if not start:
                            sp.wait_ge(f_z, i * 8)
                        sp.dma_start(hT[:, :, :], hT_v[:, :, bass.ds(i * NPI, NPI)]).then_inc(f_h, 16)
                        sp.dma_start(deg[:, :], deg_d[:, bass.ds(i * NPI, NPI)]).then_inc(f_h, 16)
                        if not start:
                            sp.wait_ge(f_hb, i * 2)
                        sp.dma_start(hin[:, :, :], hn_d[bass.ds(i * NPI, NPI), :].rearrange("(s p) c -> p s c", p=P)).then_inc(f_hin, 16)

                    over_blocks(sp, body)

                @block.tensor
                def _(pe):
                    pe.wait_ge(f_w, 48)

                    def body(i, start, end):
                        pe.wait_ge(f_s, i * 16 + 16)
                        for v in range(2):
                            for c in range(4):
                                if not start or v or c >= 2:
                                    pe.wait_ge(f_tc, i * 8 + (4 * v + c - 1))
                                for k in range(KV):
                                    mm = pe.matmul(ps_s[:, c % 2, k * W:(k + 1) * W], sst[:, KV * v + k, c * P:(c + 1) * P],
                                                   fold[:, :], start=True, stop=True)
                                mm.then_inc(f_t, 1)
                        pe.wait_ge(f_h, i * 32 + 32)
                        for v in range(2):
                            pe.wait_ge(f_tc, i * 8 + (4 * v + 4))
                            for m in range(4):
                                if not start or v or m >= 2:
                                    pe.wait_ge(f_u, i * 8 + (4 * v + m - 1))
                                z = ps_z[:, m % 2, 0:NV]
                                ms = slice(m * P, (m + 1) * P)
                                vs = slice(v * NV, (v + 1) * NV)
                                for c in range(2):
                                    pe.matmul(z, nwa[:, c, ms], hT[:, c, vs], start=c == 0, stop=False)
                                for c in range(4):
                                    pe.matmul(z, w2n[:, c, ms], sT[:, v, c, :], start=False, stop=False)
                                pe.matmul(z, b2n[:, ms], deg[:, vs], start=False, stop=True).then_inc(f_z, 1)
                        for s in range(BPI):
                            pe.wait_ge(f_u, i * 8 + (8 if (s + 1) * P > NV else 4))
                            if not start or s >= 2:
                                pe.wait_ge(f_y, i * BPI + before(s, BPI, 2))
                            for m in range(4):
                                mm = pe.matmul(ps_o[:, s % 2, 0:D], uT[:, m, s * P:(s + 1) * P], nw2[:, m, :],
                                               start=m == 0, stop=m == 3)
                            mm.then_inc(f_o, 1)

                    over_blocks(pe, body)

                @block.scalar
                def _(act):
                    act.dma_start(gam[:, :], a["gamma"].broadcast_to([P, D])).then_inc(f_gb, 16)
                    act.dma_start(bet[:, :], a["beta"].broadcast_to([P, D])).then_inc(f_gb, 16)
                    act.dma_start(nb2[:, :], a["nb2"].broadcast_to([P, D])).then_inc(f_gb, 16)
                    act.wait_ge(f_w, 48)

                    def body(i, start, end):
                        for v in range(2):
                            for c in range(4):
                                act.wait_ge(f_t, i * 8 + (4 * v + c + 1))
                                if not start:
                                    act.wait_ge(f_z, i * 8 + (4 * v - 4))
                                act.copy(sT[:, v, c, :], ps_s[:, c % 2, 0:NV]).then_inc(f_tc, 1)
                        for v in range(2):
                            for m in range(4):
                                act.wait_ge(f_z, i * 8 + (4 * v + m + 1))
                                if not start:
                                    act.wait_ge(f_o, i * BPI)
                                act.activation(uT[:, m, v * NV:(v + 1) * NV], ps_z[:, m % 2, 0:NV], ACT.Relu,
                                               bias=nb1[:, m:m + 1]).then_inc(f_u, 1)

                    over_blocks(act, body)

                @block.vector
                def _(dve):
                    def norm(i, q, src):
                        for s in range(BPI):
                            ins = dve.bn_stats(stats[:, s, :], src[:, s, :])
                        ins.then_inc(f_seq, 1)
                        dve.wait_ge(f_seq, i * 4 + (2 * q + 1))
                        gate(dve)
                        for s in range(BPI):
                            ins = dve.bn_aggr(mv[:, s, :], stats[:, s, :])
                        ins.then_inc(f_seq, 1)
                        dve.wait_ge(f_seq, i * 4 + (2 * q + 2))
                        dve.tensor_scalar(vare[:, :], mv[:, :, 1], EPS, None, ALU.add).then_inc(f_var, 1)
                        dve.wait_ge(f_rs, i * 2 + (q + 1))

                    def body(i, start, end):
                        dve.wait_ge(f_hb, i * 2 + 1)
                        if not start:
                            dve.wait_ge(f_out, i)
                        for s in range(BPI):
                            dve.wait_ge(f_o, i * BPI + (s + 1))
                            dve.tensor_tensor(y[:, s, :], ps_o[:, s % 2, 0:D], hb[:, s, :], ALU.add).then_inc(f_y, 1)
                        dve.wait_ge(f_y, i * BPI + BPI)
                        norm(i, 0, y)
                        if not start:
                            dve.wait_ge(f_st, i * 16)
                        for s in range(BPI):
                            ins = dve.tensor_scalar(y2[:, s, :], y[:, s, :], mv[:, s, 0:1], rstd[:, s:s + 1], ALU.subtract, ALU.mult)
                        ins.then_inc(f_n, 1)
                        dve.wait_ge(f_g, i * 2 + 2)
                        norm(i, 1, y)
                        for s in range(BPI):
                            ins = dve.tensor_scalar(y2[:, s, :], y[:, s, :], mv[:, s, 0:1], rstd[:, s:s + 1], ALU.subtract, ALU.mult)
                        ins.then_inc(f_out, 1)

                    over_blocks(dve, body)

                @block.gpsimd
                def _(pool):
                    pool.memset(half[:, :], -0.5).then_inc(f_half, 1)
                    pool.wait_ge(f_half, 1)
                    pool.wait_ge(f_gb, 48)

                    def body(i, start, end):
                        def row(v):
                            return v[:, None, :].broadcast_to([P, BPI, D])

                        pool.wait_ge(f_hin, i * 16 + 16)
                        if not start:
                            pool.wait_ge(f_y, i * BPI)
                        pool.tensor_tensor(hb[:, :, :], hin[:, :, :], row(nb2), ALU.add).then_inc(f_hb, 1)
                        pool.tensor_tensor(hbeta[:, :, :], hin[:, :, :], row(bet), ALU.add).then_inc(f_hb, 1)
                        pool.wait_ge(f_var, i * 2 + 1)
                        pool.tensor_tensor(rstd[:, :], vare[:, :], half[:, :], ALU.pow).then_inc(f_rs, 1)
                        pool.wait_ge(f_n, i + 1)
                        pool.tensor_tensor(y2[:, :, :], y2[:, :, :], row(gam), ALU.mult).then_inc(f_g, 1)
                        pool.wait_ge(f_g, i * 2 + 1)
                        pool.tensor_tensor(y[:, :, :], y2[:, :, :], hbeta[:, :, :], ALU.add).then_inc(f_g, 1)
                        pool.wait_ge(f_var, i * 2 + 2)
                        pool.tensor_tensor(rstd[:, :], vare[:, :], half[:, :], ALU.pow).then_inc(f_rs, 1)
                        pool.wait_ge(f_out, i + 1)
                        if not end:
                            pool.dma_start(out[bass.ds(i * NPI, NPI), :].rearrange("(s p) c -> p s c", p=P), y2[:, :, :]).then_inc(f_st, 16)
                        else:
                            left = n_nodes - (NI - 1) * NPI
                            whole = left // P
                            at = (NI - 1) * NPI
                            stores = 0
                            if whole:
                                pool.dma_start(out[at:at + whole * P, :].rearrange("(s p) c -> p s c", p=P), y2[:, 0:whole, :]).then_inc(f_st, 16)
                                stores += 1
                            if left % P:
                                pool.dma_start(out[at + whole * P:n_nodes, :], y2[0:left % P, whole, :]).then_inc(f_st, 16)
                                stores += 1
                            pool.wait_ge(f_st, 16 * (NI - 1 + stores))

                    over_blocks(pool, body)


def kernel(x, src, dst, edge_attr_64, edge_weight, L0_gnn_kernel, L0_gnn_bias, L1_gnn_eW1, L1_gnn_eb1, L1_gnn_eW2,
           L1_gnn_eb2, L1_gnn_nW1, L1_gnn_nb1, L1_gnn_nW2, L1_gnn_nb2, L1_gnn_ln_gamma, L1_gnn_ln_beta):
    import numpy as np
    import concourse.bacc as bacc
    from concourse.bass_utils import run_bass_kernel_spmd

    nodes, edges = x.shape[0], src.shape[0]
    tiles = -(-edges // (TPI * P)) * TPI
    pad = tiles * P - edges
    NP = -(-nodes // NPI) * NPI
    x = np.concatenate([np.asarray(x), np.zeros((NP - nodes, D), np.float32)])
    src = np.concatenate([np.asarray(src), np.zeros(pad, np.int32)])
    dst = np.concatenate([np.asarray(dst), np.full(pad, FAR, np.int32)])
    w = np.concatenate([np.asarray(edge_weight), np.zeros(pad, np.float32)])
    ea = np.concatenate([np.asarray(edge_attr_64), np.zeros((pad, EA), np.float32)])
    own = np.ascontiguousarray
    ins = {
        "x": x,
        "xT": own(x.T),
        "src_row": own(src[None, :]),
        "dst_row": own(dst[None, :]),
        "src_col": own(src.reshape(tiles, P).T),
        "dst_col": own(dst.reshape(tiles, P).T),
        "w_col": own(w.reshape(tiles, P).T),
        "eaT": own(ea.T),
        "K": own(L0_gnn_kernel),
        "b0": own(np.asarray(L0_gnn_bias)[None, :]),
        "eW1": own(L1_gnn_eW1),
        "eb1": own(np.asarray(L1_gnn_eb1)[None, :]),
        "eW2T": own(np.asarray(L1_gnn_eW2).T),
        "eb2_col": own(np.asarray(L1_gnn_eb2).reshape(2, P).T),
        "nW1": own(L1_gnn_nW1),
        "nb1_col": own(np.asarray(L1_gnn_nb1).reshape(4, P).T),
        "nW2": own(L1_gnn_nW2),
        "nb2": own(np.asarray(L1_gnn_nb2)[None, :]),
        "gamma": own(np.asarray(L1_gnn_ln_gamma)[None, :]),
        "beta": own(np.asarray(L1_gnn_ln_beta)[None, :]),
    }
    nc = bacc.Bacc("TRN2", target_bir_lowering=False, num_devices=1)
    aps = {n: nc.dram_tensor(f"in_{n}", v.shape, mybir.dt.from_np(v.dtype), kind="ExternalInput").ap() for n, v in ins.items()}
    out = nc.dram_tensor("out", (nodes, D), F32, kind="ExternalOutput").ap()
    build(nc, aps, out, nodes, tiles)
    return run_bass_kernel_spmd(nc, [{f"in_{n}": v for n, v in ins.items()}], core_ids=[0]).results[0]["out"]
```

```python
from contextlib import ExitStack

import concourse.bass as bass
from concourse import mybir

F32 = mybir.dt.float32
BF16 = mybir.dt.bfloat16
I32 = mybir.dt.int32
ALU = mybir.AluOpType
ACT = mybir.ActivationFunctionType
AX = mybir.AxisListType

P = 128
W = 64
TPI = 8
HT = TPI // 2
GPI = TPI // 2
TABLES = 4
D = 256
HID = 512
EA = 64
BPI = 5
NPI = BPI * P
EPS = 1e-5
FAR = 1 << 20


def build(nc, a, out, n_nodes, n_tiles):
    NG = n_tiles // 2
    NB = -(-n_nodes // NPI) * BPI
    NP = NB * P
    NK = NP // W
    NW = -(-n_nodes // W)
    TR = NP + P
    CP = NG // 2
    NI = NB // BPI

    xk_d = nc.dram_tensor("xk_scratch", (NP, D), F32, kind="Internal").ap()
    table = [nc.dram_tensor(f"table{r}_scratch", (TR, D), F32, kind="Internal").ap() for r in range(TABLES)]
    A_d = nc.dram_tensor("A_scratch", (NP, HID), F32, kind="Internal").ap()
    B_d = nc.dram_tensor("B_scratch", (NP, HID), F32, kind="Internal").ap()
    hn_d = nc.dram_tensor("h_scratch", (NP, D), F32, kind="Internal").ap()
    hT_d = nc.dram_tensor("hT_scratch", (D, NP), F32, kind="Internal").ap()
    deg_d = nc.dram_tensor("deg_scratch", (1, NP), F32, kind="Internal").ap()

    xk_f = xk_d.rearrange("n c -> (n c)")
    B_f = B_d.rearrange("n c -> (n c)")

    ctx = ExitStack()
    with ctx:
        def sb(c, name, shape, dt=F32):
            return c.enter_context(nc.sbuf_tensor(name, shape, dt))

        def pb(c, name, shape, dt=F32):
            return c.enter_context(nc.psum_tensor(name, shape, dt))

        def sem(name):
            return ctx.enter_context(nc.semaphore(name))

        def sems(name, n):
            return [sem(f"{name}{i}") for i in range(n)]

        def over_tiles(eng, body):
            body(0, True, False)
            with eng.Fori(1, n_tiles // TPI - 1) as i:
                body(eng.snap(i * TPI), False, False)
            body(n_tiles - TPI, False, True)

        def ahead(work, t, g, start, end):
            if g < GPI:
                work(t, g, start)
            elif not end:
                work(t + TPI, g - GPI, False)

        def over_blocks(eng, body, peeled=1):
            body(0, True, False)
            if NI - peeled > 1:
                with eng.Fori(1, NI - peeled) as i:
                    body(i, False, False)
            for i in range(max(1, NI - peeled), NI):
                body(i, False, i == NI - 1)

        turn = sem("turn")

        def gate(eng):
            eng.sem_inc(turn, 1)

        def before(k, per, slots):
            q = k - 1
            while (q % per) % slots != k % slots:
                q -= 1
            return q + 1

        iota = sb(ctx, "iota", [P, W])
        iota64 = sb(ctx, "iota64", [P, W])
        pid = sb(ctx, "pid", [P, 1])
        pmod = sb(ctx, "pmod", [P, 1])
        ident = sb(ctx, "ident", [P, P])
        dst_c = sb(ctx, "dst_c", [P, n_tiles])
        src_c = sb(ctx, "src_c", [P, n_tiles])
        first_b = sb(ctx, "first_b", [P, NG])
        base = sb(ctx, "base", [P, NG])
        base_i = sb(ctx, "base_i", [P, NG], I32)
        col_i = sb(ctx, "col_i", [P, NG], I32)
        res_i = sb(ctx, "res_i", [P, NG], I32)
        res = sb(ctx, "res", [P, NG])
        col = sb(ctx, "col", [P, NG])
        many_i = sb(ctx, "many_i", [P, 1], I32)
        lo = sb(ctx, "lo", [P, n_tiles])
        S = sb(ctx, "S", [P, NK, HID])

        f_w = sem("f_w")
        f_gb = sem("f_gb")
        nw1 = sb(ctx, "nw1", [P, 4, HID])
        w2 = sb(ctx, "w2", [P, 4, D])
        eb2 = sb(ctx, "eb2", [P, 2])
        nw2 = sb(ctx, "nw2", [P, 4, D])
        nb1 = sb(ctx, "nb1", [P, 4])
        gam = sb(ctx, "gam", [P, D])
        bet = sb(ctx, "bet", [P, D])
        nb2 = sb(ctx, "nb2", [P, D])

        n_w = sem("n_w")
        node_weights = ExitStack()
        wa = sb(node_weights, "wa", [P, 2, HID])
        wb = sb(node_weights, "wb", [P, 2, HID])
        eb1 = sb(node_weights, "eb1", [P, HID])

        first_layer = ExitStack()
        zero = sb(first_layer, "zero", [P, D])
        bias = sb(first_layer, "bias", [P, D])
        tri = sb(first_layer, "tri", [P, P])
        w_c = sb(first_layer, "w_c", [P, n_tiles])
        hi = sb(first_layer, "hi", [P, n_tiles])
        spare_c = sb(first_layer, "spare_c", [P, n_tiles])

        s_iota = sem("s_iota")
        s_const = sem("s_const")
        s_chk = sem("s_chk")
        s_first = sem("s_first")
        s_dst = sem("s_dst")
        s_src = sem("s_src")
        s_w = sem("s_w")
        s_tables = sems("s_tables", TABLES)
        s_bad = sem("s_bad")
        s_count = sem("s_count")
        s_zero = sem("s_zero")
        s_bias = sem("s_bias")
        s_kw = sem("s_kw")
        s_xt = sems("s_xt", BPI)
        s_xmm = sem("s_xmm")
        s_xcp = sem("s_xcp")
        s_xst = sems("s_xst", BPI)

        st = ExitStack()
        with st:
            it_i = sb(st, "it_i", [P, P], I32)
            ip_i = sb(st, "ip_i", [P, 1], I32)
            im_i = sb(st, "im_i", [P, 1], I32)
            ones = sb(st, "ones", [P, P])
            dci = sb(st, "dci", [P, n_tiles], I32)
            sci = sb(st, "sci", [P, n_tiles], I32)
            chk = sb(st, "chk", [CP, 2, 2 * P], I32)
            real = sb(st, "real", [CP, 2, 2 * P])
            mn = sb(st, "mn", [CP, 2])
            mx = sb(st, "mx", [CP, 2])
            below = sb(st, "below", [CP, 2])
            last = sb(st, "last", [CP, 2])
            above = sb(st, "above", [CP, 2])
            either = sb(st, "either", [CP, 2])
            bad = sb(st, "bad", [CP, 1])
            first_i = sb(st, "first_i", [1, NG], I32)
            first = sb(st, "first", [1, NG])
            fast = sb(st, "fast", [P, 1])
            many = sb(st, "many", [P, 1])
            kw = sb(st, "kw", [P, 2, D])
            xt = sb(st, "xt", [P, BPI, 2, P])
            xo = sb(st, "xo", [P, BPI, D])
            lo_i = sb(st, "lo_i", [P, n_tiles], I32)
            hi_i = sb(st, "hi_i", [P, n_tiles], I32)
            ps_x = pb(st, "ps_x", [P, 2, 512])
            ps_b = pb(st, "ps_b", [P, 512])
            ps_c = pb(st, "ps_c", [P, 512])

            with nc.Block() as block:
                @block.sync
                def _(sp):
                    xT = a["xT"].rearrange("(c p) n -> p c n", p=P)

                    def body(i, start, end):
                        for s in range(BPI):
                            if not start:
                                sp.wait_ge(s_xmm, i * BPI + (s + 1 - BPI))
                            sp.dma_start(xt[:, s, :, :], xT[:, :, bass.ds(i * NPI + s * P, P)]).then_inc(s_xt[s], 16)

                    sp.dma_start(kw[:, :, :], a["K"].rearrange("(c p) n -> p c n", p=P)).then_inc(s_kw, 16)
                    sp.dma_start(chk[:, :, :], a["dst_row"].rearrange("o (p g e) -> (o p) g e", g=2, e=2 * P)).then_inc(s_chk, 16)
                    sp.dma_start(first_i[:, :], a["dst_row"][:, 0:n_tiles * P:2 * P], allow_slow_non_contiguous=True).then_inc(s_first, 16)
                    sp.dma_start(dci[:, :], a["dst_col"]).then_inc(s_dst, 16)
                    sp.dma_start(sci[:, :], a["src_col"]).then_inc(s_src, 16)
                    sp.dma_start(w_c[:, :], a["w_col"]).then_inc(s_w, 16)
                    over_blocks(sp, body)
                    sp.wait_ge(s_zero, 1)
                    for r in range(TABLES // 2, TABLES):
                        sp.dma_start(table[r].rearrange("(p n) c -> p n c", p=P),
                                     zero[:, None, :].broadcast_to([P, TR // P, D])).then_inc(s_tables[r], 16)
                    sp.wait_ge(s_w, 16)

                @block.scalar
                def _(act):
                    act.dma_start(bias[:, :], a["b0"].broadcast_to([P, D])).then_inc(s_bias, 16)
                    act.wait_ge(s_zero, 1)
                    act.wait_ge(s_bias, 16)
                    for r in range(TABLES // 2):
                        fill = (zero if r else bias)[:, :]
                        act.dma_start(table[r].rearrange("(p n) c -> p n c", p=P),
                                      fill[:, None, :].broadcast_to([P, TR // P, D])).then_inc(s_tables[r], 16)

                    def body(i, start, end):
                        for s in range(BPI):
                            act.wait_ge(s_xmm, i * BPI + (s + 1))
                            if not start:
                                act.wait_ge(s_xst[s], i * 16)
                            act.copy(xo[:, s, :], ps_x[:, s % 2, 0:D]).then_inc(s_xcp, 1)

                    over_blocks(act, body)

                @block.gpsimd
                def _(pool):
                    pool.iota(it_i[:, :], [[1, P]], base=0, channel_multiplier=0).then_inc(s_iota, 1)
                    pool.iota(ip_i[:, :], [[0, 1]], base=0, channel_multiplier=1).then_inc(s_iota, 1)
                    pool.memset(zero[:, :], 0.0).then_inc(s_zero, 1)

                    def body(i, start, end):
                        for s in range(BPI):
                            pool.wait_ge(s_xcp, i * BPI + (s + 1))
                            pool.dma_start(xk_d[bass.ds(i * NPI + s * P, P), :], xo[:, s, :]).then_inc(s_xst[s], 16)

                    over_blocks(pool, body)
                    for s in range(BPI):
                        pool.wait_ge(s_xst[s], 16 * NI)

                @block.tensor
                def _(pe):
                    pe.wait_ge(s_kw, 16)

                    def body(i, start, end):
                        for s in range(BPI):
                            pe.wait_ge(s_xt[s], i * 16 + 16)
                            if not start or s >= 2:
                                pe.wait_ge(s_xcp, i * BPI + before(s, BPI, 2))
                            for c in range(2):
                                mm = pe.matmul(ps_x[:, s % 2, 0:D], xt[:, s, c, :], kw[:, c, :], start=c == 0, stop=c == 1)
                            mm.then_inc(s_xmm, 1)

                    over_blocks(pe, body)
                    pe.wait_ge(s_bad, 1)
                    pe.matmul(ps_c[:, 0:1], ones[0:CP, :], bad[:, :], start=True, stop=True).then_inc(s_count, 1)
                    pe.wait_ge(s_bad, 2)
                    pe.matmul(ps_b[:, 0:NG], ones[0:1, :], first[:, :], start=True, stop=True).then_inc(s_count, 1)

                @block.vector
                def _(dve):
                    done = [0]

                    def step(ins):
                        done[0] += 1
                        ins.then_inc(s_const, 1)
                        dve.wait_ge(s_const, done[0])

                    dve.memset(ones[:, :], 1.0)
                    dve.memset(S[:, :, :], 0.0)
                    dve.wait_ge(s_iota, 2)
                    dve.tensor_copy(iota[:, :], it_i[:, 0:W])
                    dve.tensor_copy(pid[:, :], ip_i[:, :])
                    step(dve.tensor_scalar(im_i[:, :], ip_i[:, :], W - 1, None, ALU.bitwise_and))
                    dve.tensor_scalar(iota64[:, :], iota[:, :], 1.0 / W, None, ALU.mult)
                    step(dve.tensor_copy(pmod[:, :], im_i[:, :]))
                    dve.tensor_scalar(ident[:, :], it_i[:, :], pid[:, :], None, ALU.is_equal)
                    dve.tensor_scalar(tri[:, :], it_i[:, :], pid[:, :], None, ALU.is_lt)
                    dve.wait_ge(s_chk, 16)
                    dve.tensor_reduce(mn[:, :], chk[:, :, :], AX.X, ALU.min)
                    step(dve.scalar_tensor_tensor(real[:, :, :], chk[:, :, :], float(NP), chk[:, :, :], ALU.is_lt, ALU.mult))
                    dve.tensor_reduce(mx[:, :], real[:, :, :], AX.X, ALU.max)
                    step(dve.tensor_scalar(last[:, :], chk[:, :, 0], float(W - 1), None, ALU.add))
                    dve.tensor_tensor(below[:, :], mn[:, :], chk[:, :, 0], ALU.is_lt)
                    step(dve.tensor_tensor(above[:, :], mx[:, :], last[:, :], ALU.is_gt))
                    step(dve.tensor_tensor(either[:, :], below[:, :], above[:, :], ALU.add))
                    dve.tensor_reduce(bad[:, :], either[:, :], AX.X, ALU.add).then_inc(s_bad, 1)
                    dve.wait_ge(s_first, 16)
                    dve.tensor_copy(first[:, :], first_i[:, :]).then_inc(s_bad, 1)
                    dve.wait_ge(s_dst, 16)
                    dve.tensor_copy(dst_c[:, :], dci[:, :])
                    dve.wait_ge(s_src, 16)
                    step(dve.tensor_copy(src_c[:, :], sci[:, :]))
                    dve.tensor_scalar(spare_c[:, :], src_c[:, :], pid[:, :], -1.0, ALU.subtract, ALU.mult)
                    dve.wait_ge(s_count, 1)
                    dve.tensor_scalar(fast[:, :], ps_c[:, 0:1], 0.5, None, ALU.is_lt)
                    step(dve.tensor_scalar(many[:, :], ps_c[:, 0:1], 0.5, None, ALU.is_gt))
                    dve.tensor_copy(many_i[:, :], many[:, :])
                    dve.wait_ge(s_count, 2)
                    dve.tensor_scalar(first_b[:, :], ps_b[:, 0:NG], fast[:, :], None, ALU.mult)
                    step(dve.tensor_scalar(spare_c[:, :], spare_c[:, :], float(NP), None, ALU.add))
                    dve.tensor_scalar(lo_i[:, :], dci[:, :], W - 1, None, ALU.bitwise_and)
                    step(dve.tensor_scalar(hi_i[:, :], dci[:, :], 6, None, ALU.arith_shift_right))
                    dve.tensor_copy(lo[:, :], lo_i[:, :])
                    dve.tensor_copy(hi[:, :], hi_i[:, :])

        def window_tables(dve, s_tab, first_pass, more):
            seq = [0]

            def step(ins):
                seq[0] += 1
                ins.then_inc(s_tab, 1)
                dve.wait_ge(s_tab, seq[0])

            if first_pass:
                step(dve.tensor_copy(base[:, :], first_b[:, :]))
            else:
                step(dve.tensor_scalar(base[:, :], base[:, :], float(W), None, ALU.add))
            step(dve.tensor_copy(base_i[:, :], base[:, :]))
            dve.tensor_scalar(col_i[:, :], base_i[:, :], 6, None, ALU.arith_shift_right)
            step(dve.tensor_scalar(res_i[:, :], base_i[:, :], W - 1, None, ALU.bitwise_and))
            step(dve.tensor_copy(res[:, :], res_i[:, :]))
            step(dve.tensor_tensor(col[:, :], base[:, :], res[:, :], ALU.subtract))
            more(step)
            return seq[0]

        c_tab = sem("c_tab")
        c_srow = sems("c_srow", 2)
        c_win = sems("c_win", GPI)
        c_hot = sem("c_hot")
        c_pick = sem("c_pick")
        c_pickc = sem("c_pickc")
        c_msg = sem("c_msg")
        c_msgc = sem("c_msgc")
        c_dup = sem("c_dup")
        c_idx = sem("c_idx")
        c_add = sems("c_add", TPI)
        c_zero = sem("c_zero")
        c_digit = sem("c_digit")
        c_count = sem("c_count")
        c_deg = sem("c_deg")
        c_degt = sem("c_degt")
        c_degst = sem("c_degst")

        def neighbour_sum(first_pass):
            st = ExitStack()
            with st:
                tag = "a" if first_pass else "b"
                srow = sb(st, "srow_n" + tag, [P, TPI, P], I32)
                win = sb(st, "win_n" + tag, [P, GPI, D])
                rel = sb(st, "rel_n" + tag, [P, n_tiles])
                whot = sb(st, "whot_n" + tag, [P, TPI, P])
                same = sb(st, "same_n" + tag, [P, TPI, P])
                junk = sb(st, "junk_n" + tag, [P, TPI, P])
                dup = sb(st, "dup_n" + tag, [P, TPI])
                jump = sb(st, "jump_n" + tag, [P, TPI])
                idx = sb(st, "idx_n" + tag, [P, TPI], I32)
                pick = sb(st, "pick_n" + tag, [P, TPI, P])
                lohot = sb(st, "lohot" + tag, [P, TPI, W], BF16)
                hihot = sb(st, "hihot" + tag, [P, TPI, NK], BF16)
                none = sb(st, "none" + tag, [P, W], BF16)
                degc = sb(st, "degc" + tag, [W, NK])
                degr = sb(st, "degr" + tag, [NK, W])
                msg = sb(st, "msg_n" + tag, [P, TPI, D])
                ps_p = pb(st, "ps_p_n" + tag, [P, 2, HT * P])
                ps_m = pb(st, "ps_m_n" + tag, [P, TPI // 2, 2 * D])
                ps_d = pb(st, "ps_d" + tag, [P, 512])
                ps_t = pb(st, "ps_t" + tag, [P, 512])
                NTAB = 6

                with nc.Block() as block:
                    @block.sync
                    def _(sp):
                        sp.wait_ge(c_tab, NTAB)

                        def body(t, start, end):
                            for hh in range(2):
                                if not start:
                                    sp.wait_ge(c_dup, t + HT * hh + HT - TPI)
                                sp.dma_start(srow[:, HT * hh:HT * hh + HT, :],
                                             a["src_row"][:, bass.ds(t * P + HT * hh * P, HT * P)]
                                             .rearrange("o (j e) -> o j e", e=P).broadcast_to([P, HT, P])).then_inc(c_srow[hh], 16)
                                for g in (2 * hh, 2 * hh + 1):
                                    at = sp.snap(sp.value_load(base_i[0:1, bass.ds(t // 2 + g, 1)], min_val=0, max_val=NP - W) * D)
                                    if not start:
                                        sp.wait_ge(c_msg, t + 2 * g + 2 - TPI)
                                    sp.dma_start(win[0:W, g, :], xk_f[bass.ds(at, W * D)].rearrange("(n c) -> n c", c=D)).then_inc(c_win[g], 16)
                            if end and first_pass:
                                sp.dma_start(wa[:, :, :], a["eW1"][0:D, :].rearrange("(c p) n -> p c n", p=P)).then_inc(n_w, 16)
                                sp.dma_start(wb[:, :, :], a["eW1"][D:2 * D, :].rearrange("(c p) n -> p c n", p=P)).then_inc(n_w, 16)
                                sp.dma_start(eb1[:, :], a["eb1"].broadcast_to([P, HID])).then_inc(n_w, 16)

                        over_tiles(sp, body)
                        if first_pass:
                            sp.wait_ge(c_deg, 2)
                            sp.dma_start(deg_d.rearrange("o (k r) -> (o k) r", r=W), degr[:, :]).then_inc(c_degst, 16)
                            sp.wait_ge(c_degst, 16)

                    @block.vector
                    def _(dve):
                        def more(step):
                            step(dve.tensor_tensor(rel[:, :].rearrange("p (g j) -> p g j", j=2),
                                                   dst_c[:, :].rearrange("p (g j) -> p g j", j=2),
                                                   base[:, :, None].broadcast_to([P, NG, 2]), ALU.subtract))

                        dve.memset(whot[:, :, W:P], 0.0)
                        dve.memset(none[:, :], 0.0).then_inc(c_zero, 1)
                        window_tables(dve, c_tab, first_pass, more)

                        def body(t, start, end):
                            for hh in range(2):
                                dve.wait_ge(c_srow[hh], t * 2 + 16)
                                for j in range(HT * hh, HT * hh + HT):
                                    at = bass.ds(t + j, 1)
                                    if not start:
                                        dve.wait_ge(c_pick, t + j + 1 - TPI)
                                    dve.tensor_scalar(whot[:, j, 0:W], iota[:, :], rel[:, at], w_c[:, at], ALU.is_equal, ALU.mult)
                                    dve.tensor_scalar(same[:, j, :], srow[:, j, :], src_c[:, at], None,
                                                      ALU.is_equal).then_inc(c_hot, 1)
                                    dve.scalar_tensor_tensor(junk[:, j, :], srow[:, j, :], src_c[:, at], tri[:, :], ALU.is_equal,
                                                             ALU.mult, accum_out=dup[:, j:j + 1]).then_inc(c_dup, 1)
                                js = slice(HT * hh, HT * hh + HT)
                                cols = bass.ds(t + HT * hh, HT)
                                if first_pass:
                                    if not start:
                                        dve.wait_ge(c_count, t + HT * hh + HT - TPI)
                                    dve.tensor_tensor(lohot[:, js, :], iota[:, None, 0:W].broadcast_to([P, HT, W]),
                                                      lo[:, cols][:, :, None].broadcast_to([P, HT, W]), ALU.is_equal)
                                    dve.tensor_tensor(hihot[:, js, :], iota[:, None, 0:NK].broadcast_to([P, HT, NK]),
                                                      hi[:, cols][:, :, None].broadcast_to([P, HT, NK]),
                                                      ALU.is_equal).then_inc(c_digit, HT)
                                dve.wait_ge(c_dup, t + HT * hh + HT)
                                dve.scalar_tensor_tensor(jump[:, js], dup[:, js], 1.0, spare_c[:, cols], ALU.min,
                                                         ALU.mult).then_inc(c_tab, 1)
                                dve.wait_ge(c_tab, jumps(t, hh))
                                if not start:
                                    for j in range(HT * hh, HT * hh + HT):
                                        dve.wait_ge(c_add[j], t * 2)
                                dve.tensor_tensor(idx[:, js], jump[:, js], src_c[:, cols], ALU.add).then_inc(c_idx, HT)

                        def jumps(t, hh):
                            return t // HT + (NTAB + hh + 1)

                        over_tiles(dve, body)
                        if first_pass:
                            dve.wait_ge(c_count, n_tiles + 1)
                            dve.tensor_copy(degc[:, :], ps_d[0:W, 0:NK]).then_inc(c_deg, 1)
                            dve.wait_ge(c_degt, 1)
                            dve.tensor_copy(degr[:, :], ps_t[0:NK, 0:W]).then_inc(c_deg, 1)

                    @block.tensor
                    def _(pe):
                        pe.wait_ge(c_zero, 2)
                        if first_pass:
                            pe.matmul(ps_d[0:W, 0:NK], none[:, :], none[:, 0:NK], start=True, stop=False)

                        def body(t, start, end):
                            for hh in range(2):
                                if not start:
                                    pe.wait_ge(c_pickc, t + HT * hh + HT - TPI)
                                for j in range(HT * hh, HT * hh + HT):
                                    pe.wait_ge(c_hot, t + j + 1)
                                    pe.matmul(ps_p[:, hh, (j % HT) * P:(j % HT + 1) * P], whot[:, j, :], same[:, j, :],
                                              start=True, stop=True).then_inc(c_pick, 1)
                                if first_pass:
                                    pe.wait_ge(c_digit, t + HT * hh + HT)
                                    for j in range(HT * hh, HT * hh + HT):
                                        mm = pe.matmul(ps_d[0:W, 0:NK], lohot[:, j, :], hihot[:, j, :], start=False, stop=False)
                                    mm.then_inc(c_count, HT)
                                pe.wait_ge(c_pickc, t + HT * hh + HT)
                                for j in range(HT * hh, HT * hh + HT):
                                    if j % 2 == 0:
                                        pe.wait_ge(c_win[j // 2], t * 2 + 16)
                                        if not start:
                                            pe.wait_ge(c_msgc, t + j + 2 - TPI)
                                    pe.matmul(ps_m[:, j // 2, (j % 2) * D:(j % 2 + 1) * D], pick[:, j, :], win[:, j // 2, :],
                                              start=True, stop=True).then_inc(c_msg, 1)

                        over_tiles(pe, body)
                        if first_pass:
                            pe.matmul(ps_d[0:W, 0:NK], none[:, :], none[:, 0:NK], start=False, stop=True).then_inc(c_count, 1)
                            pe.wait_ge(c_deg, 1)
                            pe.transpose(ps_t[0:NK, 0:W], degc[:, :], ident[0:W, 0:W]).then_inc(c_degt, 1)

                    @block.scalar
                    def _(act):
                        def body(t, start, end):
                            for hh in range(2):
                                act.wait_ge(c_pick, t + HT * hh + HT)
                                if not start:
                                    act.wait_ge(c_msg, t + HT * hh + HT - TPI)
                                act.copy(pick[:, HT * hh:HT * hh + HT, :],
                                         ps_p[:, hh, :].rearrange("p (j e) -> p j e", e=P)).then_inc(c_pickc, HT)
                                for q in (2 * hh, 2 * hh + 1):
                                    act.wait_ge(c_msg, t + 2 * q + 2)
                                    if not start:
                                        for j in (2 * q, 2 * q + 1):
                                            act.wait_ge(c_add[j], t * 2)
                                    act.copy(msg[:, 2 * q:2 * q + 2, :],
                                             ps_m[:, q, :].rearrange("p (j c) -> p j c", c=D)).then_inc(c_msgc, 2)

                        over_tiles(act, body)

                    @block.gpsimd
                    def _(pool):
                        def body(t, start, end):
                            for j in range(TPI):
                                if j % 2 == 0:
                                    pool.wait_ge(c_msgc, t + j + 2)
                                if j % HT == 0:
                                    pool.wait_ge(c_idx, t + j + HT)
                                if j >= TABLES:
                                    pool.wait_ge(c_add[j - TABLES], t * 2 + 16)
                                elif not start:
                                    pool.wait_ge(c_add[j - TABLES + TPI], t * 2)
                                else:
                                    pool.wait_ge(s_tables[j], 16)
                                gate(pool)
                                pool.indirect_dma_start(table[j % TABLES][:, :], bass.IndirectOffsetOnAxis(ap=idx[:, j:j + 1], axis=0),
                                                        msg[:, j, :], None, compute_op=ALU.add).then_inc(c_add[j], 16)

                        pool.memset(win[W:P, :, :], 0.0).then_inc(c_zero, 1)
                        over_tiles(pool, body)
                        for j in range(TPI):
                            pool.wait_ge(c_add[j], 2 * n_tiles)

        pass_sems = [c_tab, *c_srow, *c_win, c_hot, c_pick, c_pickc, c_msg, c_msgc, c_dup, c_idx, *c_add, c_zero, c_digit,
                     c_count, c_deg, c_degt, c_degst]

        def clear(which):
            numbers = range(min(s.num for s in which), max(s.num for s in which) + 1)
            with nc.Block() as block:
                @block.gpsimd
                def _(pool):
                    pool.dma_reset(numbers)

                @block.sync
                def _(sp):
                    sp.drain(semaphore_range=numbers)
            with nc.Block() as block:
                @block.gpsimd
                def _(pool):
                    pool.sem_clear(numbers)

        def over_windows(one_pass, which):
            one_pass(True)
            again = nc.values_load(many_i[0:1, 0:1], min_val=0, max_val=1)
            with nc.If(again > 0):
                with nc.Fori(1, NW) as _w:
                    clear(which)
                    one_pass(False)

        over_windows(neighbour_sum, pass_sems)
        first_layer.close()

        n_half = sem("n_half")
        n_in = sems("n_in", TABLES)
        n_x = sem("n_x")
        n_acc = sem("n_acc")
        n_sum = sem("n_sum")
        n_var = sem("n_var")
        n_rs = sem("n_rs")
        n_h = sem("n_h")
        n_t = sem("n_t")
        n_tc = sem("n_tc")
        n_ab = sem("n_ab")
        n_abc = sem("n_abc")
        n_b = sem("n_b")
        n_st = sems("n_st", BPI)

        st = ExitStack()
        with st:
            half = sb(st, "half", [P, BPI])
            part = sb(st, "part", [P, TABLES, BPI, D])
            xin = sb(st, "xin", [P, BPI, D])
            acc = sb(st, "acc", [P, BPI, D])
            pre = sb(st, "pre", [P, BPI, D])
            stats = sb(st, "stats", [P, BPI, 6])
            mv = sb(st, "mv", [P, BPI, 2])
            vare = sb(st, "vare", [P, BPI])
            rstd = sb(st, "rstd", [P, BPI])
            h = sb(st, "h", [P, BPI, D])
            hT = sb(st, "hT", [P, BPI, 2, P])
            ao = sb(st, "ao", [P, BPI, HID])
            bo = sb(st, "bo", [P, BPI, HID])
            ps_t = pb(st, "ps_th", [P, 2, 512])
            ps_ab = pb(st, "ps_ab", [P, 4, HID])

            with nc.Block() as block:
                @block.gpsimd
                def _(pool):
                    pool.memset(half[:, :], -0.5).then_inc(n_half, 1)

                    def root(i):
                        pool.wait_ge(n_var, i + 1)
                        if not isinstance(i, int) or i:
                            pool.wait_ge(n_h, i * BPI)
                        pool.tensor_tensor(rstd[:, :], vare[:, :], half[:, :], ALU.pow).then_inc(n_rs, 1)

                    pool.wait_ge(n_half, 1)
                    root(0)
                    pool.wait_ge(n_w, 48)

                    def body(i, start, end):
                        for s in range(BPI):
                            if s == 3 and not end:
                                root(i + 1)
                            pool.wait_ge(n_abc, i * (2 * BPI) + (2 * s + 2))
                            pool.tensor_tensor(bo[:, s, :], bo[:, s, :], eb1[:, :], ALU.add).then_inc(n_b, 1)

                    over_blocks(pool, body)

                @block.vector
                def _(dve):
                    def sum_tables(i):
                        for r in range(1, TABLES):
                            dve.wait_ge(n_in[r], i * 16 + 16)
                            if r == 1:
                                dve.wait_ge(n_in[0], i * 16 + 16)
                            dve.tensor_tensor(acc[:, :, :], part[:, r, :, :], part[:, 0, :, :] if r == 1 else acc[:, :, :],
                                              ALU.add).then_inc(n_acc, 1)
                            dve.wait_ge(n_acc, i * (TABLES - 1) + r)

                    sum_tables(0)

                    def body(i, start, end):
                        if not start:
                            dve.wait_ge(n_h, i * BPI)
                        dve.wait_ge(n_x, i * 16 + 16)
                        dve.scalar_tensor_tensor(pre[:, :, :], acc[:, :, :], 0.0, xin[:, :, :], ALU.max, ALU.add).then_inc(n_sum, 1)
                        dve.wait_ge(n_sum, i * 3 + 1)
                        for s in range(BPI):
                            ins = dve.bn_stats(stats[:, s, :], pre[:, s, :])
                        ins.then_inc(n_sum, 1)
                        dve.wait_ge(n_sum, i * 3 + 2)
                        gate(dve)
                        for s in range(BPI):
                            ins = dve.bn_aggr(mv[:, s, :], stats[:, s, :])
                        ins.then_inc(n_sum, 1)
                        dve.wait_ge(n_sum, i * 3 + 3)
                        dve.tensor_scalar(vare[:, :], mv[:, :, 1], EPS, None, ALU.add).then_inc(n_var, 1)
                        dve.wait_ge(n_rs, i + 1)
                        for s in range(BPI):
                            if s == 3 and not end:
                                sum_tables(i + 1)
                            if not start:
                                dve.wait_ge(n_t, i * BPI + (s + 1 - BPI))
                                dve.wait_ge(n_st[s], i * 64)
                            dve.tensor_scalar(h[:, s, :], pre[:, s, :], mv[:, s, 0:1], rstd[:, s:s + 1], ALU.subtract,
                                              ALU.mult).then_inc(n_h, 1)

                    over_blocks(dve, body)

                @block.tensor
                def _(pe):
                    pe.wait_ge(n_w, 48)

                    def transposes(i, s, start):
                        pe.wait_ge(n_h, i * BPI + (s + 1))
                        if not start or s >= 2:
                            pe.wait_ge(n_tc, i * BPI + before(s, BPI, 2))
                        for c in range(2):
                            mm = pe.transpose(ps_t[:, s % 2, c * P:(c + 1) * P], h[:, s, c * P:(c + 1) * P], ident[:, :])
                        mm.then_inc(n_t, 1)

                    def products(i, s, start):
                        pe.wait_ge(n_tc, i * BPI + (s + 1))
                        for z, w in enumerate((wa, wb)):
                            slot = (2 * s + z) % 4
                            if not start or s >= 2:
                                pe.wait_ge(n_abc, i * (2 * BPI) + before(2 * s + z, 2 * BPI, 4))
                            for c in range(2):
                                mm = pe.matmul(ps_ab[:, slot, :], hT[:, s, c, :], w[:, c, :], start=c == 0, stop=c == 1)
                            mm.then_inc(n_ab, 1)

                    def body(i, start, end):
                        transposes(i, 0, start)
                        for s in range(BPI):
                            if s + 1 < BPI:
                                transposes(i, s + 1, start)
                            products(i, s, start)

                    over_blocks(pe, body)

                @block.scalar
                def _(act):
                    def transposed(i, s, start):
                        act.wait_ge(n_t, i * BPI + (s + 1))
                        if not start:
                            act.wait_ge(n_ab, i * (2 * BPI) + (2 * s + 2 - 2 * BPI))
                            act.wait_ge(n_st[s], i * 64)
                        act.copy(hT[:, s, :, :], ps_t[:, s % 2, 0:2 * P].rearrange("p (c n) -> p c n", c=2)).then_inc(n_tc, 1)

                    def body(i, start, end):
                        transposed(i, 0, start)
                        for s in range(BPI):
                            if s + 1 < BPI:
                                transposed(i, s + 1, start)
                            for z in range(2):
                                act.wait_ge(n_ab, i * (2 * BPI) + (2 * s + z + 1))
                                act.copy((bo if z else ao)[:, s, :], ps_ab[:, (2 * s + z) % 4, :]).then_inc(n_abc, 1)

                    over_blocks(act, body)

                @block.sync
                def _(sp):
                    hT_v = hT_d.rearrange("(c p) n -> p c n", p=P)

                    def load(i):
                        for r in range(TABLES):
                            sp.dma_start(part[:, r, :, :], table[r][bass.ds(i * NPI, NPI), :].rearrange("(s p) c -> p s c", p=P)).then_inc(n_in[r], 16)

                    def load_x(i):
                        sp.dma_start(xin[:, :, :], a["x"][bass.ds(i * NPI, NPI), :].rearrange("(s p) c -> p s c", p=P)).then_inc(n_x, 16)

                    load(0)
                    load_x(0)
                    sp.wait_ge(n_acc, TABLES - 1)
                    load(1)

                    def body(i, start, end):
                        for s in range(BPI):
                            if s == 0 and not end:
                                sp.wait_ge(n_var, i + 1)
                                load_x(i + 1)
                            if s == 3 and not (isinstance(i, int) and i + 2 >= NI):
                                sp.wait_ge(n_acc, i * (TABLES - 1) + 2 * (TABLES - 1))
                                load(i + 2)
                            rows = bass.ds(i * NPI + s * P, P)
                            sp.wait_ge(n_tc, i * BPI + (s + 1))
                            sp.dma_start(hT_v[:, :, rows], hT[:, s, :, :]).then_inc(n_st[s], 16)
                            sp.wait_ge(n_h, i * BPI + (s + 1))
                            sp.dma_start(hn_d[rows, :], h[:, s, :]).then_inc(n_st[s], 16)
                            sp.wait_ge(n_abc, i * (2 * BPI) + (2 * s + 1))
                            sp.dma_start(A_d[rows, :], ao[:, s, :]).then_inc(n_st[s], 16)
                            sp.wait_ge(n_b, i * BPI + (s + 1))
                            sp.dma_start(B_d[rows, :], bo[:, s, :]).then_inc(n_st[s], 16)

                    over_blocks(sp, body, peeled=2)
                    for s in range(BPI):
                        sp.wait_ge(n_st[s], 64 * NI)
        node_weights.close()

        m_tab = sem("m_tab")
        m_wc = sem("m_wc")
        m_ea = sems("m_ea", 2)
        m_drow = sems("m_drow", 2)
        m_idx = sem("m_idx")
        m_win = sems("m_win", GPI)
        m_gat = sems("m_gat", TPI)
        m_row = sem("m_row")
        m_hot = sem("m_hot")
        m_hots = sem("m_hots")
        m_pre = sem("m_pre")
        m_copy = sem("m_copy")
        m_relu = sem("m_relu")
        m_agg = sem("m_agg")
        m_out = sem("m_out")

        def message_sum(first_pass):
            st = ExitStack()
            with st:
                tag = "a" if first_pass else "b"
                lhs = sb(st, "lhs_m" + tag, [P, TPI, P])
                rhs = sb(st, "rhs_m" + tag, [P, GPI, HID])
                drow = sb(st, "drow_m" + tag, [W, TPI, P], I32)
                gidx = sb(st, "gidx_m" + tag, [P, TPI], I32)
                winid = sb(st, "winid_m" + tag, [P, NG])
                rel = sb(st, "rel_m" + tag, [P, n_tiles])
                below = sb(st, "below_m" + tag, [P, NG])
                above = sb(st, "above_m" + tag, [P, NG])
                wrow = sb(st, "wrow_m" + tag, [P, GPI, W])
                hot = sb(st, "hot_m" + tag, [P, TPI, W])
                pre = sb(st, "pre_m" + tag, [P, TPI, HID])
                hid = sb(st, "hid_m" + tag, [P, TPI, HID])
                ps_p = pb(st, "ps_p_m" + tag, [P, HT, HID])
                ps_a = pb(st, "ps_a_m" + tag, [P, GPI, HID])
                pack = sb(st, "pack_m" + tag, [P, NG])
                pack_i = sb(st, "pack_i_m" + tag, [P, NG], I32)

                with nc.Block() as block:
                    @block.sync
                    def _(sp):
                        for g in range(GPI):
                            sp.dma_start(rhs[W:P, g, :], a["eW1"][2 * D:2 * D + EA, :]).then_inc(m_wc, 16)
                        sp.wait_ge(m_tab, 3)

                        def body(t, start, end):
                            for hh in range(2):
                                js = slice(HT * hh, HT * hh + HT)
                                edges = bass.ds(t * P + HT * hh * P, HT * P)
                                if not start:
                                    sp.wait_ge(m_hot, t + HT * hh + HT - TPI)
                                sp.dma_start(drow[:, js, :], a["dst_row"][:, edges].rearrange("o (j e) -> o j e", e=P)
                                             .broadcast_to([W, HT, P])).then_inc(m_drow[hh], 16)
                                at = [sp.snap(sp.value_load(base_i[0:1, bass.ds(t // 2 + g, 1)], min_val=0, max_val=NP - W) * HID)
                                      for g in (2 * hh, 2 * hh + 1)]
                                if not start:
                                    sp.wait_ge(m_pre, t + HT * hh + HT - TPI)
                                sp.dma_start(lhs[W:P, js, :], a["eaT"][:, edges].rearrange("f (j e) -> f j e", e=P)).then_inc(m_ea[hh], 16)
                                for g in (2 * hh, 2 * hh + 1):
                                    sp.dma_start(rhs[0:W, g, :], B_f[bass.ds(at[g % 2], W * HID)].rearrange("(n c) -> n c", c=HID)
                                                 ).then_inc(m_win[g], 16)
                            if end and first_pass:
                                sp.dma_start(nw1[:, :, :], a["nW1"].rearrange("(c p) n -> p c n", p=P)).then_inc(f_w, 16)
                                sp.dma_start(w2[:, :, :], a["eW2"].rearrange("(c p) n -> p c n", p=P)).then_inc(f_w, 16)
                                sp.dma_start(eb2[:, :], a["eb2_col"]).then_inc(f_w, 16)
                                sp.dma_start(nw2[:, :, :], a["nW2"].rearrange("(c p) n -> p c n", p=P)).then_inc(f_w, 16)
                                sp.dma_start(nb1[:, :], a["nb1_col"]).then_inc(f_w, 16)
                                sp.dma_start(gam[:, :], a["gamma"].broadcast_to([P, D])).then_inc(f_gb, 16)
                                sp.dma_start(bet[:, :], a["beta"].broadcast_to([P, D])).then_inc(f_gb, 16)
                                sp.dma_start(nb2[:, :], a["nb2"].broadcast_to([P, D])).then_inc(f_gb, 16)

                        over_tiles(sp, body)

                    @block.gpsimd
                    def _(pool):
                        def body(t, start, end):
                            for j in range(TPI):
                                if j % 2 == 0:
                                    pool.wait_ge(m_idx, t + j + 2)
                                pool.wait_ge(m_copy, t + j + 1)
                                gate(pool)
                                pool.indirect_dma_start(pre[:, j, :], None, A_d[:, :],
                                                        bass.IndirectOffsetOnAxis(ap=gidx[:, j:j + 1], axis=0),
                                                        compute_op=ALU.add).then_inc(m_gat[j], 16)

                        over_tiles(pool, body)

                    @block.vector
                    def _(dve):
                        def more(step):
                            step(dve.tensor_scalar(winid[:, :], base[:, :], pid[:, :], None, ALU.add))
                            step(dve.tensor_tensor(rel[:, :].rearrange("p (g j) -> p g j", j=2),
                                                   dst_c[:, :].rearrange("p (g j) -> p g j", j=2),
                                                   col[:, :, None].broadcast_to([P, NG, 2]), ALU.subtract))
                            step(dve.tensor_scalar(rel[:, :], rel[:, :], 1.0 / W, None, ALU.mult))
                            step(dve.tensor_scalar(above[:, :], res[:, :], pmod[:, :], None, ALU.is_le))
                            step(dve.tensor_scalar(below[:, :], res[:, :], pmod[:, :], None, ALU.is_gt))
                            for k in (2, 1, 0):
                                step(dve.scalar_tensor_tensor(pack[:, 0:NG - 3], col[:, 3:NG] if k == 2 else pack[:, 0:NG - 3],
                                                              float(W), col[:, k:NG - 3 + k], ALU.mult, ALU.add))
                            step(dve.tensor_copy(pack_i[:, 0:NG - 3], pack[:, 0:NG - 3]))

                        window_tables(dve, m_tab, first_pass, more)

                        def columns(group):
                            v = dve.value_load(pack_i[0:1, bass.ds(group, 1)], min_val=0, max_val=(1 << 30) - 1)
                            return [dve.snap(nc.s_assert_within(
                                (v >> (6 * k + 6)) & (W - 1), 0, NK - 2,
                                skip_runtime_bounds_check_because="col is kept within S by window_tables")) for k in range(4)]

                        def pick_hots(t, g, start):
                            if g % 2 == 0:
                                dve.wait_ge(m_drow[g // 2], t * 2 + 16)
                            if not start:
                                dve.wait_ge(m_pre, t + 2 * g + 2 - TPI)
                            dve.tensor_scalar(lhs[0:W, 2 * g:2 * g + 2, :], drow[:, 2 * g:2 * g + 2, :],
                                              winid[0:W, bass.ds(t // 2 + g, 1)], None, ALU.is_equal).then_inc(m_hot, 2)

                        def node_rows(t, g, start):
                            if not start:
                                dve.wait_ge(m_hots, t + 2 * g + 2 - TPI)
                            dve.scalar_tensor_tensor(wrow[:, g, :], iota[:, :], res[:, bass.ds(t // 2 + g, 1)], iota64[:, :],
                                                     ALU.is_lt, ALU.add).then_inc(m_row, 1)

                        def sum_hots(t, g, start):
                            if not start:
                                dve.wait_ge(m_agg, t + 2 * g + 2 - TPI)
                            dve.wait_ge(m_row, t // 2 + (g + 1))
                            for j in (2 * g, 2 * g + 1):
                                dve.tensor_scalar(hot[:, j, :], wrow[:, g, :], rel[:, bass.ds(t + j, 1)], None,
                                                  ALU.is_equal).then_inc(m_hots, 1)

                        def to_s(at, t, g, start):
                            grp = bass.ds(t // 2 + g, 1)
                            dve.wait_ge(m_agg, t + 2 * g + 2)
                            if not start or g:
                                dve.wait_ge(m_out, t + 2 * g)
                            dve.scalar_tensor_tensor(S[:, bass.ds(at, 1), :], ps_a[:, g:g + 1, :], above[:, grp],
                                                     S[:, bass.ds(at, 1), :], ALU.mult, ALU.add).then_inc(m_out, 1)
                            dve.scalar_tensor_tensor(S[:, bass.ds(at + 1, 1), :], ps_a[:, g:g + 1, :], below[:, grp],
                                                     S[:, bass.ds(at + 1, 1), :], ALU.mult, ALU.add).then_inc(m_out, 1)

                        for g in range(GPI):
                            pick_hots(0, g, True)
                        node_rows(0, 0, True)
                        node_rows(0, 1, True)
                        sum_hots(0, 0, True)

                        def body(t, start, end):
                            at = [None] + columns(0) if start else columns(t // 2 - 1)
                            for g in range(GPI):
                                ahead(pick_hots, t, g + 4, start, end)
                                ahead(node_rows, t, g + 2, start, end)
                                ahead(sum_hots, t, g + 1, start, end)
                                if g:
                                    to_s(at[g], t, g - 1, start)
                                elif not start:
                                    to_s(at[0], t - TPI, GPI - 1, False)

                        over_tiles(dve, body)
                        last_at = dve.value_load(col_i[0:1, NG - 1:NG], min_val=0, max_val=NK - 2)
                        to_s(last_at, n_tiles - TPI, GPI - 1, False)

                    @block.scalar
                    def _(act):
                        def copies(t, g, start):
                            for j in (2 * g, 2 * g + 1):
                                act.wait_ge(m_pre, t + j + 1)
                                if not start:
                                    act.wait_ge(m_relu, t + j + 1 - TPI)
                                act.copy(pre[:, j, :], ps_p[:, j % HT, :]).then_inc(m_copy, 1)

                        def relus(t, g, start):
                            for j in (2 * g, 2 * g + 1):
                                act.wait_ge(m_gat[j], t * 2 + 16)
                                if not start:
                                    act.wait_ge(m_agg, t + j + 1 - TPI)
                                act.activation(hid[:, j, :], pre[:, j, :], ACT.Relu).then_inc(m_relu, 1)

                        def indices(t, g):
                            act.copy(gidx[:, 2 * g:2 * g + 2], src_c[:, bass.ds(t + 2 * g, 2)]).then_inc(m_idx, 2)

                        for g in range(GPI):
                            indices(0, g)
                            copies(0, g, True)

                        def body(t, start, end):
                            for g in range(GPI):
                                relus(t, g, start)
                                if not end:
                                    indices(t + TPI, g)
                                    copies(t + TPI, g, False)

                        over_tiles(act, body)

                    @block.tensor
                    def _(pe):
                        pe.wait_ge(m_wc, 16 * GPI)

                        def products(t, g, start):
                            if g % 2 == 0:
                                pe.wait_ge(m_ea[g // 2], t * 2 + 16)
                            pe.wait_ge(m_win[g], t * 2 + 16)
                            pe.wait_ge(m_hot, t + 2 * g + 2)
                            for j in (2 * g, 2 * g + 1):
                                if not start or j >= HT:
                                    pe.wait_ge(m_copy, t + j + 1 - HT)
                                pe.matmul(ps_p[:, j % HT, :], lhs[:, j, :], rhs[:, g, :], start=True, stop=True).then_inc(m_pre, 1)

                        def sums(t, g, start):
                            if not start:
                                pe.wait_ge(m_out, t + 2 * g + 2 - TPI)
                            pe.wait_ge(m_hots, t + 2 * g + 2)
                            for j in (2 * g, 2 * g + 1):
                                pe.wait_ge(m_relu, t + j + 1)
                                q = W * (j % 2)
                                pe.matmul(ps_a[q:q + W, g, :], hot[:, j, :], hid[:, j, :], start=True, stop=True).then_inc(m_agg, 1)

                        for g in range(GPI):
                            products(0, g, True)

                        def body(t, start, end):
                            for g in range(GPI):
                                ahead(products, t, g + 4, start, end)
                                sums(t, g, start)

                        over_tiles(pe, body)

        over_windows(message_sum, [m_tab, m_wc, *m_ea, *m_drow, m_idx, *m_win, *m_gat, m_row, m_hot, m_hots, m_pre, m_copy,
                                   m_relu, m_agg, m_out])

        f_half = sem("f_half")
        f_s = sem("f_s")
        f_h = sem("f_h")
        f_hin = sem("f_hin")
        f_hb = sem("f_hb")
        f_t = sem("f_t")
        f_tc = sem("f_tc")
        f_ts = sem("f_ts")
        f_g4 = sem("f_g4")
        f_a = sem("f_a")
        f_z = sem("f_z")
        f_u = sem("f_u")
        f_o = sem("f_o")
        f_y = sem("f_y")
        f_seq = sem("f_seq")
        f_var = sem("f_var")
        f_rs = sem("f_rs")
        f_n = sem("f_n")
        f_out = sem("f_out")
        f_st = sem("f_st")
        NV = NPI // 2
        KV = NV // W

        st = ExitStack()
        with st:
            half = sb(st, "half2", [P, BPI])
            sst = sb(st, "sst", [P, 2 * KV, HID])
            hT = sb(st, "hT2", [P, 2, NPI])
            deg = sb(st, "deg2", [P, NPI])
            aT = sb(st, "aT", [P, 2, NPI])
            hin = sb(st, "hin", [P, BPI, D])
            hbeta = sb(st, "hbeta", [P, BPI, D])
            sT = sb(st, "sT", [P, 2, 4, NV])
            uT = sb(st, "uT", [P, 4, NPI])
            y = sb(st, "y", [P, BPI, D])
            y2 = sb(st, "y2", [P, BPI, D])
            stats = sb(st, "stats2", [P, BPI, 6])
            mv = sb(st, "mv2", [P, BPI, 2])
            vare = sb(st, "vare2", [P, BPI])
            rstd = sb(st, "rstd2", [P, BPI])
            ps_s = pb(st, "ps_s", [P, 2, 1024])
            ps_z = pb(st, "ps_z", [P, 2, 512])
            ps_o = pb(st, "ps_o", [P, 2, 512])

            with nc.Block() as block:
                @block.sync
                def _(sp):
                    hT_v = hT_d.rearrange("(c p) n -> p c n", p=P)

                    def body(i, start, end):
                        if not start and not end:
                            sp.wait_ge(f_t, i * 8)
                            sp.dma_start(sst[:, :, :], S[:, bass.ds(i * (2 * KV), 2 * KV), :]).then_inc(f_s, 16)
                        if not start:
                            sp.wait_ge(f_z, i * 8)
                            gate(sp)
                            sp.wait_ge(f_a, i * 4)
                        sp.dma_start(hT[:, :, :], hT_v[:, :, bass.ds(i * NPI, NPI)]).then_inc(f_h, 16)
                        sp.dma_start(deg[:, :], deg_d[:, bass.ds(i * NPI, NPI)].broadcast_to([P, NPI])).then_inc(f_h, 16)
                        if not start:
                            sp.wait_ge(f_y, i * BPI)
                        sp.dma_start(hin[:, :, :], hn_d[bass.ds(i * NPI, NPI), :].rearrange("(s p) c -> p s c", p=P)).then_inc(f_hin, 16)

                    over_blocks(sp, body)

                @block.tensor
                def _(pe):
                    pe.wait_ge(f_w, 80)

                    def body(i, start, end):
                        if start or end:
                            cols = S[:, i * 2 * KV:(i + 1) * 2 * KV, :]
                        else:
                            cols = sst
                            pe.wait_ge(f_s, i * 16)
                        for v in range(2):
                            for c in range(4):
                                if not start or v or c >= 2:
                                    pe.wait_ge(f_ts, i * 8 + (4 * v + c - 1))
                                for k in range(KV):
                                    mm = pe.transpose(ps_s[:, c % 2, k * P:(k + 1) * P],
                                                      cols[:, KV * v + k, c * P:(c + 1) * P], ident[:, :])
                                mm.then_inc(f_t, 1)
                        for v in range(2):
                            pe.wait_ge(f_ts, i * 8 + (4 * v + 4))
                            for f in range(2):
                                if v:
                                    pe.wait_ge(f_a, i * 4 + (f + 1))
                                elif not start:
                                    pe.wait_ge(f_u, i * 8 + (f - 1))
                                for c in range(4):
                                    mm = pe.matmul(ps_z[:, f, 0:NV], w2[:, c, f * P:(f + 1) * P], sT[:, v, c, :],
                                                   start=c == 0, stop=c == 3)
                                mm.then_inc(f_g4, 1)
                        pe.wait_ge(f_h, i * 32 + 32)
                        for v in range(2):
                            for m in range(4):
                                if v == 0 and m < 2:
                                    pe.wait_ge(f_a, i * 4 + (m + 3))
                                else:
                                    pe.wait_ge(f_u, i * 8 + (4 * v + m - 1))
                                if v:
                                    pe.wait_ge(f_a, i * 4 + 4)
                                for c in range(4):
                                    src = hT if c < 2 else aT
                                    mm = pe.matmul(ps_z[:, m % 2, 0:NV], nw1[:, c, m * P:(m + 1) * P],
                                                   src[:, c % 2, v * NV:(v + 1) * NV], start=c == 0, stop=c == 3)
                                mm.then_inc(f_z, 1)
                        for s in range(BPI):
                            pe.wait_ge(f_u, i * 8 + (8 if (s + 1) * P > NV else 4))
                            if not start or s >= 2:
                                pe.wait_ge(f_y, i * BPI + before(s, BPI, 2))
                            for m in range(4):
                                mm = pe.matmul(ps_o[:, s % 2, 0:D], uT[:, m, s * P:(s + 1) * P], nw2[:, m, :],
                                               start=m == 0, stop=m == 3)
                            mm.then_inc(f_o, 1)

                    over_blocks(pe, body)

                @block.scalar
                def _(act):
                    act.wait_ge(f_w, 80)

                    def body(i, start, end):
                        for v in range(2):
                            for c in range(4):
                                act.wait_ge(f_t, i * 8 + (4 * v + c + 1))
                                if not start:
                                    act.wait_ge(f_g4, i * 4 + (2 * v - 2))
                                act.copy(sT[:, v, c, :].rearrange("p (k n) -> p k n", n=W),
                                         ps_s[:, c % 2, 0:KV * P].rearrange("p (k n) -> p k n", n=P)[:, :, 0:W]).then_inc(f_tc, 1)
                        for v in range(2):
                            for m in range(4):
                                act.wait_ge(f_z, i * 8 + (4 * v + m + 1))
                                if not start:
                                    act.wait_ge(f_o, i * BPI)
                                act.activation(uT[:, m, v * NV:(v + 1) * NV], ps_z[:, m % 2, 0:NV], ACT.Relu,
                                               bias=nb1[:, m:m + 1]).then_inc(f_u, 1)

                    over_blocks(act, body)

                @block.vector
                def _(dve):
                    dve.wait_ge(f_gb, 48)

                    def norm(i, q, src):
                        for s in range(BPI):
                            ins = dve.bn_stats(stats[:, s, :], src[:, s, :])
                        ins.then_inc(f_seq, 1)
                        dve.wait_ge(f_seq, i * 4 + (2 * q + 1))
                        gate(dve)
                        for s in range(BPI):
                            ins = dve.bn_aggr(mv[:, s, :], stats[:, s, :])
                        ins.then_inc(f_seq, 1)
                        dve.wait_ge(f_seq, i * 4 + (2 * q + 2))
                        dve.tensor_scalar(vare[:, :], mv[:, :, 1], EPS, None, ALU.add).then_inc(f_var, 1)

                    def norms(i):
                        dve.wait_ge(f_y, i * BPI + BPI)
                        norm(i, 0, y)
                        for s in range(BPI):
                            ins = dve.scalar_tensor_tensor(y2[:, s, :], y[:, s, :], mv[:, s, 0:1], gam[:, :], ALU.subtract, ALU.mult)
                        ins.then_inc(f_n, 1)
                        dve.wait_ge(f_n, i * 2 + 1)
                        dve.wait_ge(f_rs, i * 2 + 1)
                        for s in range(BPI):
                            ins = dve.scalar_tensor_tensor(y[:, s, :], y2[:, s, :], rstd[:, s:s + 1], hbeta[:, s, :], ALU.mult, ALU.add)
                        ins.then_inc(f_n, 1)
                        dve.wait_ge(f_n, i * 2 + 2)
                        norm(i, 1, y)
                        dve.wait_ge(f_rs, i * 2 + 2)
                        for s in range(BPI):
                            ins = dve.tensor_scalar(y2[:, s, :], y[:, s, :], mv[:, s, 0:1], rstd[:, s:s + 1], ALU.subtract, ALU.mult)
                        ins.then_inc(f_out, 1)

                    def body(i, start, end):
                        for v in range(2):
                            for c in range(4):
                                dve.wait_ge(f_tc, i * 8 + (4 * v + c + 1))
                                half_t = sT[:, v, c, :].rearrange("p (k n) -> p k n", n=W)
                                dve.tensor_tensor(half_t, ps_s[:, c % 2, 0:KV * P].rearrange("p (k n) -> p k n", n=P)[:, :, W:P],
                                                  half_t, ALU.add).then_inc(f_ts, 1)
                        dve.wait_ge(f_h, i * 32 + 32)
                        if not start:
                            dve.wait_ge(f_z, i * 8)
                        for v in range(2):
                            for f in range(2):
                                dve.wait_ge(f_g4, i * 4 + (2 * v + f + 1))
                                dve.scalar_tensor_tensor(aT[:, f, v * NV:(v + 1) * NV], deg[:, v * NV:(v + 1) * NV], eb2[:, f:f + 1],
                                                         ps_z[:, f, 0:NV], ALU.mult, ALU.add).then_inc(f_a, 1)
                        if not start:
                            norms(i - 1)
                            dve.wait_ge(f_out, i)
                        dve.wait_ge(f_hb, i * 2 + 2)
                        for s in range(BPI):
                            dve.wait_ge(f_o, i * BPI + (s + 1))
                            dve.tensor_tensor(y[:, s, :], ps_o[:, s % 2, 0:D], hin[:, s, :], ALU.add).then_inc(f_y, 1)
                        if not start:
                            dve.wait_ge(f_st, i * 16)

                    over_blocks(dve, body)
                    norms(NI - 1)

                @block.gpsimd
                def _(pool):
                    pool.memset(half[:, :], -0.5).then_inc(f_half, 1)
                    pool.wait_ge(f_half, 1)
                    pool.wait_ge(f_gb, 48)

                    def row(v):
                        return v[:, None, :].broadcast_to([P, BPI, D])

                    def norms(i, end):
                        pool.wait_ge(f_var, i * 2 + 1)
                        pool.tensor_tensor(rstd[:, :], vare[:, :], half[:, :], ALU.pow).then_inc(f_rs, 1)
                        pool.wait_ge(f_var, i * 2 + 2)
                        pool.tensor_tensor(rstd[:, :], vare[:, :], half[:, :], ALU.pow).then_inc(f_rs, 1)
                        pool.wait_ge(f_out, i + 1)
                        if not end:
                            pool.dma_start(out[bass.ds(i * NPI, NPI), :].rearrange("(s p) c -> p s c", p=P), y2[:, :, :]).then_inc(f_st, 16)
                        else:
                            left = n_nodes - (NI - 1) * NPI
                            whole = left // P
                            at = (NI - 1) * NPI
                            stores = 0
                            if whole:
                                pool.dma_start(out[at:at + whole * P, :].rearrange("(s p) c -> p s c", p=P), y2[:, 0:whole, :]).then_inc(f_st, 16)
                                stores += 1
                            if left % P:
                                pool.dma_start(out[at + whole * P:n_nodes, :], y2[0:left % P, whole, :]).then_inc(f_st, 16)
                                stores += 1
                            pool.wait_ge(f_st, 16 * (NI - 1 + stores))

                    def body(i, start, end):
                        if not start:
                            norms(i - 1, False)
                        pool.wait_ge(f_hin, i * 16 + 16)
                        pool.tensor_tensor(hbeta[:, :, :], hin[:, :, :], row(bet), ALU.add).then_inc(f_hb, 1)
                        pool.wait_ge(f_hb, i * 2 + 1)
                        pool.tensor_tensor(hin[:, :, :], hin[:, :, :], row(nb2), ALU.add).then_inc(f_hb, 1)

                    over_blocks(pool, body)
                    norms(NI - 1, True)


def kernel(x, src, dst, edge_attr_64, edge_weight, L0_gnn_kernel, L0_gnn_bias, L1_gnn_eW1, L1_gnn_eb1, L1_gnn_eW2,
           L1_gnn_eb2, L1_gnn_nW1, L1_gnn_nb1, L1_gnn_nW2, L1_gnn_nb2, L1_gnn_ln_gamma, L1_gnn_ln_beta):
    import numpy as np
    import concourse.bacc as bacc
    from concourse.bass_utils import run_bass_kernel_spmd

    nodes, edges = x.shape[0], src.shape[0]
    tiles = -(-edges // (TPI * P)) * TPI
    pad = tiles * P - edges
    NP = -(-nodes // NPI) * NPI
    x = np.concatenate([np.asarray(x), np.zeros((NP - nodes, D), np.float32)])
    src = np.concatenate([np.asarray(src), np.zeros(pad, np.int32)])
    dst = np.concatenate([np.asarray(dst), np.full(pad, FAR, np.int32)])
    w = np.concatenate([np.asarray(edge_weight), np.zeros(pad, np.float32)])
    ea = np.concatenate([np.asarray(edge_attr_64), np.zeros((pad, EA), np.float32)])
    own = np.ascontiguousarray
    ins = {
        "x": x,
        "xT": own(x.T),
        "src_row": own(src[None, :]),
        "dst_row": own(dst[None, :]),
        "src_col": own(src.reshape(tiles, P).T),
        "dst_col": own(dst.reshape(tiles, P).T),
        "w_col": own(w.reshape(tiles, P).T),
        "eaT": own(ea.T),
        "K": own(L0_gnn_kernel),
        "b0": own(np.asarray(L0_gnn_bias)[None, :]),
        "eW1": own(L1_gnn_eW1),
        "eb1": own(np.asarray(L1_gnn_eb1)[None, :]),
        "eW2": own(L1_gnn_eW2),
        "eb2_col": own(np.asarray(L1_gnn_eb2).reshape(2, P).T),
        "nW1": own(L1_gnn_nW1),
        "nb1_col": own(np.asarray(L1_gnn_nb1).reshape(4, P).T),
        "nW2": own(L1_gnn_nW2),
        "nb2": own(np.asarray(L1_gnn_nb2)[None, :]),
        "gamma": own(np.asarray(L1_gnn_ln_gamma)[None, :]),
        "beta": own(np.asarray(L1_gnn_ln_beta)[None, :]),
    }
    nc = bacc.Bacc("TRN2", target_bir_lowering=False, num_devices=1)
    aps = {n: nc.dram_tensor(f"in_{n}", v.shape, mybir.dt.from_np(v.dtype), kind="ExternalInput").ap() for n, v in ins.items()}
    out = nc.dram_tensor("out", (nodes, D), F32, kind="ExternalOutput").ap()
    build(nc, aps, out, nodes, tiles)
    return run_bass_kernel_spmd(nc, [{f"in_{n}": v for n, v in ins.items()}], core_ids=[0]).results[0]["out"]
```
